# Optimizing a Trainium2 kernel written in Bass

```python
import numpy as np
import jax
import jax.numpy as jnp

def _softmax(x, axis=-1):
    return jax.nn.softmax(x, axis=axis)

def _gelu(x):
    return jax.nn.gelu(x, approximate=True)

def _silu(x):
    return jax.nn.silu(x)

def _sigmoid(x):
    return jax.nn.sigmoid(x)

def _layernorm(x, axis=-1, eps=1e-05):
    m = jnp.mean(x, axis=axis, keepdims=True)
    v = jnp.var(x, axis=axis, keepdims=True)
    return (x - m) / jnp.sqrt(v + eps)

def _scatter_add(tgt, idx, src, axis=0):
    return tgt.at[idx].add(src)

def _segment_sum(src, seg, n):
    return jax.ops.segment_sum(src, seg, n)
kernel_name = 'mk_hybrid_d1_jaxref_r8_8c02e3'

def setup_inputs(seed: int=0):
    np.random.seed(seed)
    _w = jnp.asarray

    def _L0_attn_a_setup():
        import jax, jax.numpy as jnp
        import numpy as np
        DIM = 128
        HEADS = 16
        HEAD_DIM = DIM // HEADS
        ROPE_BASE = 500000.0
        SCALE = HEAD_DIM ** (-0.5)

        def _rope_cos_sin(T, dtype=jnp.float32):
            inv_freq = 1.0 / ROPE_BASE ** (jnp.arange(0, HEAD_DIM, 2, dtype=jnp.float32) / HEAD_DIM)
            t = jnp.arange(T, dtype=jnp.float32)
            freqs = t[:, None] * inv_freq[None, :]
            emb = jnp.concatenate([freqs, freqs], axis=-1)
            return (jnp.cos(emb).astype(dtype), jnp.sin(emb).astype(dtype))

        def _rotate_half(x):
            x1, x2 = jnp.split(x, 2, axis=-1)
            return jnp.concatenate([-x2, x1], axis=-1)

        def _apply_rope(x, cos, sin):
            return x * cos + _rotate_half(x) * sin
        key = jax.random.key(seed)
        k1, k2, k3 = jax.random.split(key, 3)
        B, T = (4, 512)
        x = jax.random.normal(k1, (B, T, DIM), dtype=jnp.float32)
        W_qkv = jax.random.normal(k2, (DIM, 3 * DIM), dtype=jnp.float32) * DIM ** (-0.5)
        W_out = jax.random.normal(k3, (DIM, DIM), dtype=jnp.float32) * DIM ** (-0.5)
        return {'x': x, 'W_qkv': W_qkv, 'W_out': W_out}
    _L0_attn_a_in = _L0_attn_a_setup()

    def _L0_attn_b_setup():
        import jax, jax.numpy as jnp
        import numpy as np
        D_MODEL = 128
        N_HEAD = 16
        HEAD_DIM = D_MODEL // N_HEAD
        EPS = 1e-06
        B, T = (4, 128)

        def _eml(x, agg, eps=EPS):
            return jnp.log(jnp.abs(x) + eps) - jnp.log(agg + eps)

        def _split_heads(t):
            b, s, _ = t.shape
            return t.reshape(b, s, N_HEAD, HEAD_DIM).transpose(0, 2, 1, 3)
        key = jax.random.key(seed)
        k0, k1, k2, k3 = jax.random.split(key, 4)
        x = jax.random.normal(k0, (B, T, D_MODEL), dtype=jnp.float32)
        bound = 0.1 / np.sqrt(D_MODEL)
        w_qkv = jax.random.uniform(k1, (3 * D_MODEL, D_MODEL), jnp.float32, -bound, bound)
        w_ky = jax.random.uniform(k2, (D_MODEL, D_MODEL), jnp.float32, -bound, bound)
        w_proj = jax.random.uniform(k3, (D_MODEL, D_MODEL), jnp.float32, -bound, bound)
        return {'x': x, 'w_qkv': w_qkv, 'w_ky': w_ky, 'w_proj': w_proj}
    _L0_attn_b_in = _L0_attn_b_setup()

    def _L0_ffn_setup():
        import jax, jax.numpy as jnp
        import numpy as np
        H = 128
        I = 256
        E = 8
        TOP_K = 2
        NUM_SHARED = 1
        key = jax.random.key(seed)
        ks = jax.random.split(key, 9)
        s = 0.02
        x = jax.random.normal(ks[0], (2, 256, H), dtype=jnp.float32)
        sg_w = jax.random.normal(ks[1], (I, H), dtype=jnp.float32) * s
        su_w = jax.random.normal(ks[2], (I, H), dtype=jnp.float32) * s
        sd_w = jax.random.normal(ks[3], (H, I), dtype=jnp.float32) * s
        router_w = jax.random.normal(ks[4], (E, H), dtype=jnp.float32) * s
        routing_bias = jnp.zeros((E,), dtype=jnp.float32)
        wg = jax.random.normal(ks[5], (E, I, H), dtype=jnp.float32) * s
        wu = jax.random.normal(ks[6], (E, I, H), dtype=jnp.float32) * s
        wd = jax.random.normal(ks[7], (E, H, I), dtype=jnp.float32) * s
        return {'x': x, 'sg_w': sg_w, 'su_w': su_w, 'sd_w': sd_w, 'router_w': router_w, 'routing_bias': routing_bias, 'wg': wg, 'wu': wu, 'wd': wd}
    _L0_ffn_in = _L0_ffn_setup()
    _d = {'L0_attn_a_x': _L0_attn_a_in['x'], 'L0_attn_a_W_qkv': _L0_attn_a_in['W_qkv'], 'L0_attn_a_W_out': _L0_attn_a_in['W_out'], 'L0_attn_b_w_qkv': _L0_attn_b_in['w_qkv'], 'L0_attn_b_w_ky': _L0_attn_b_in['w_ky'], 'L0_attn_b_w_proj': _L0_attn_b_in['w_proj'], 'L0_ffn_sg_w': _L0_ffn_in['sg_w'], 'L0_ffn_su_w': _L0_ffn_in['su_w'], 'L0_ffn_sd_w': _L0_ffn_in['sd_w'], 'L0_ffn_router_w': _L0_ffn_in['router_w'], 'L0_ffn_routing_bias': _L0_ffn_in['routing_bias'], 'L0_ffn_wg': _L0_ffn_in['wg'], 'L0_ffn_wu': _L0_ffn_in['wu'], 'L0_ffn_wd': _L0_ffn_in['wd']}
    _x0 = _d['L0_attn_a_x']
    _d['L0_attn_a_x'] = jax.random.normal(jax.random.fold_in(jax.random.key(seed), 1), (8, 512, 128), dtype=_x0.dtype)
    del _x0
    return _d

def reference(L0_attn_a_x, L0_attn_a_W_qkv, L0_attn_a_W_out, L0_attn_b_w_qkv, L0_attn_b_w_ky, L0_attn_b_w_proj, L0_ffn_sg_w, L0_ffn_su_w, L0_ffn_sd_w, L0_ffn_router_w, L0_ffn_routing_bias, L0_ffn_wg, L0_ffn_wu, L0_ffn_wd):

    def _L0_attn_a_ref(x, W_qkv, W_out):
        import jax, jax.numpy as jnp
        import numpy as np
        DIM = 128
        HEADS = 16
        HEAD_DIM = DIM // HEADS
        ROPE_BASE = 500000.0
        SCALE = HEAD_DIM ** (-0.5)

        def _rope_cos_sin(T, dtype=jnp.float32):
            inv_freq = 1.0 / ROPE_BASE ** (jnp.arange(0, HEAD_DIM, 2, dtype=jnp.float32) / HEAD_DIM)
            t = jnp.arange(T, dtype=jnp.float32)
            freqs = t[:, None] * inv_freq[None, :]
            emb = jnp.concatenate([freqs, freqs], axis=-1)
            return (jnp.cos(emb).astype(dtype), jnp.sin(emb).astype(dtype))

        def _rotate_half(x):
            x1, x2 = jnp.split(x, 2, axis=-1)
            return jnp.concatenate([-x2, x1], axis=-1)

        def _apply_rope(x, cos, sin):
            return x * cos + _rotate_half(x) * sin
        B, T, D = x.shape
        H, hd = (HEADS, HEAD_DIM)
        qkv = (x @ W_qkv).reshape(B, T, 3, H, hd).transpose(2, 0, 3, 1, 4)
        q, k, v = (qkv[0], qkv[1], qkv[2])
        cos, sin = _rope_cos_sin(T, q.dtype)
        q = _apply_rope(q, cos, sin)
        k = _apply_rope(k, cos, sin)
        q_feat = jax.nn.elu(q * SCALE) + 1.0
        k_feat = jax.nn.elu(k) + 1.0
        kv = jnp.einsum('bhtd,bhtv->bhdv', k_feat, v)
        k_sum = k_feat.sum(axis=2)
        denom = jnp.maximum(jnp.einsum('bhtd,bhd->bht', q_feat, k_sum), 1e-06)
        out = jnp.einsum('bhtd,bhdv->bhtv', q_feat, kv) / denom[..., None]
        out = out.transpose(0, 2, 1, 3).reshape(B, T, D)
        return out @ W_out

    def _L0_attn_b_ref(x, w_qkv, w_ky, w_proj):
        import jax, jax.numpy as jnp
        import numpy as np
        D_MODEL = 128
        N_HEAD = 16
        HEAD_DIM = D_MODEL // N_HEAD
        EPS = 1e-06
        B, T = (4, 128)

        def _eml(x, agg, eps=EPS):
            return jnp.log(jnp.abs(x) + eps) - jnp.log(agg + eps)

        def _split_heads(t):
            b, s, _ = t.shape
            return t.reshape(b, s, N_HEAD, HEAD_DIM).transpose(0, 2, 1, 3)
        b, t, _ = x.shape
        qkv = x @ w_qkv.T
        q, k, v = jnp.split(qkv, 3, axis=-1)
        q, k, v = (_split_heads(q), _split_heads(k), _split_heads(v))
        scale = 1.0 / np.sqrt(HEAD_DIM)
        L = jnp.einsum('bhqd,bhkd->bhqk', q, k) * scale
        mask = jnp.tril(jnp.ones((t, t), dtype=L.dtype))[None, None]
        k_y = _split_heads(x @ w_ky.T)
        L_y = jnp.einsum('bhqd,bhkd->bhqk', q, k_y) * scale
        agg = jnp.sum(jnp.exp(jnp.clip(L_y, -15.0, 15.0)) * mask, axis=-1, keepdims=True) + EPS
        r = _eml(L, agg)
        w = jax.nn.softplus(r) * mask
        A = w / (jnp.sum(w, axis=-1, keepdims=True) + EPS)
        out = jnp.einsum('bhqk,bhkd->bhqd', A, v)
        out = out.transpose(0, 2, 1, 3).reshape(b, t, D_MODEL)
        return out @ w_proj.T

    def _L0_ffn_ref(x, sg_w, su_w, sd_w, router_w, routing_bias, wg, wu, wd):
        import jax, jax.numpy as jnp
        import numpy as np
        H = 128
        I = 256
        E = 8
        TOP_K = 2
        NUM_SHARED = 1
        orig_shape = x.shape
        xt = x.reshape(-1, H)
        T = xt.shape[0]
        shared = jax.nn.silu(xt @ sg_w.T) * (xt @ su_w.T) @ sd_w.T
        shared = shared / NUM_SHARED
        logits = xt @ router_w.T + routing_bias
        probs = jax.nn.sigmoid(logits)
        topk_p, topk_idx = jax.lax.top_k(probs, TOP_K)
        topk_p = topk_p / jnp.sum(topk_p, axis=-1, keepdims=True)
        w = jnp.zeros((T, E), dtype=xt.dtype)
        w = w.at[jnp.arange(T)[:, None], topk_idx].add(topk_p)
        g = jnp.einsum('th,eih->tei', xt, wg)
        u = jnp.einsum('th,eih->tei', xt, wu)
        h = jax.nn.silu(g) * u
        y = jnp.einsum('tei,ehi->teh', h, wd)
        routed = jnp.einsum('te,teh->th', w, y)
        return (shared + routed).reshape(orig_shape)
    x = L0_attn_a_x
    x = x + _L0_attn_a_ref(_layernorm(x, axis=-1), L0_attn_a_W_qkv, L0_attn_a_W_out)
    x = x + _L0_ffn_ref(_layernorm(x, axis=-1), L0_ffn_sg_w, L0_ffn_su_w, L0_ffn_sd_w, L0_ffn_router_w, L0_ffn_routing_bias, L0_ffn_wg, L0_ffn_wu, L0_ffn_wd)
    x = x + _L0_attn_b_ref(_layernorm(x, axis=-1), L0_attn_b_w_qkv, L0_attn_b_w_ky, L0_attn_b_w_proj)
    x = x + _L0_ffn_ref(_layernorm(x, axis=-1), L0_ffn_sg_w, L0_ffn_su_w, L0_ffn_sd_w, L0_ffn_router_w, L0_ffn_routing_bias, L0_ffn_wg, L0_ffn_wu, L0_ffn_wd)
    return x

_drawn_inputs = setup_inputs


def setup_inputs(seed=0):
    import zlib

    import numpy as np

    out = dict(_drawn_inputs(seed))
    spreads = {'L0_ffn_routing_bias': (0.0, 0.8)}
    factors = {'L0_attn_b_w_qkv': 8.0,
     'L0_attn_b_w_ky': 8.0,
     'L0_attn_b_w_proj': 8.0,
     'L0_ffn_sg_w': 3.325,
     'L0_ffn_su_w': 3.231,
     'L0_ffn_sd_w': 3.201,
     'L0_ffn_router_w': 5.828,
     'L0_ffn_wg': 4.838,
     'L0_ffn_wu': 4.81,
     'L0_ffn_wd': 4.795}
    for name, (base, spread) in spreads.items():
        noise = np.random.default_rng([zlib.crc32(name.encode()), seed]).standard_normal(out[name].shape)
        drawn = base * np.exp(spread * noise) if base else spread * noise
        out[name] = jnp.asarray(drawn.astype(out[name].dtype))
    for name, factor in factors.items():
        out[name] = (out[name] * factor).astype(out[name].dtype)
    return out
```

```python
from contextlib import ExitStack

import numpy as np

import concourse.bass as bass
from concourse import mybir

F32 = mybir.dt.float32
ALU = mybir.AluOpType
ACT = mybir.ActivationFunctionType
AX = mybir.AxisListType

B, T, D = 8, 512, 128
H, HD = 16, 8
TT = T // 128
E, INNER = 9, 256
IC = INNER // 128
ROUTED = E - 1
SCALE = HD ** -0.5
LN_EPS = 1e-5
EPS = 1e-6
CLIP_LO, CLIP_HI = float(np.exp(np.float32(-15.0))), float(np.exp(np.float32(15.0)))
ROPE_BASE = 500000.0
GROUPS = H // 4
HALF = H // 2
OW = HALF * HD + HALF
OT = 2 * OW


def shape_constants():
    inv_freq = (1.0 / ROPE_BASE ** (np.arange(0, HD, 2, dtype=np.float32) / HD)).astype(np.float32)
    freqs = np.arange(T, dtype=np.float32)[:, None] * inv_freq[None, :]
    emb = np.concatenate([freqs, freqs], axis=-1).astype(np.float32)
    sign = np.where(np.arange(HD) < HD // 2, -1.0, 1.0).astype(np.float32)
    cos = np.tile(np.cos(emb), (1, H)).astype(np.float32)
    sin = np.tile(np.sin(emb) * sign, (1, H)).astype(np.float32)
    tables = {
        "rope_q": np.stack([cos.T * np.float32(SCALE), sin.T * np.float32(SCALE)], 1),
        "rope_k": np.stack([cos.reshape(TT, 128, D), sin.reshape(TT, 128, D)], 0)
        .transpose(2, 0, 1, 3),
        "identity": np.eye(128, dtype=np.float32),
    }
    head_of = np.arange(D) // HD
    tables["same_head"] = (head_of[:, None] == head_of[None, :]).astype(np.float32)
    tables["head_mask"] = (head_of[:, None] == np.arange(H)[None, :]).astype(np.float32)
    tables["head_scale"] = tables["head_mask"] * np.float32(SCALE)
    tables["choice_rank"] = np.tile(np.arange(ROUTED, 0, -1, dtype=np.float32), (128, TT))
    return {k: np.ascontiguousarray(v, dtype=np.float32).reshape(v.shape[0], -1) for k, v in tables.items()}


CONSTANTS = {"rope_q": 2 * T, "rope_k": 2 * TT * D, "identity": 128, "same_head": D, "head_mask": H,
             "head_scale": H,
             "choice_rank": TT * ROUTED}
WEIGHTS = {"w_qk_rot": 2 * D, "w_qkv": 3 * D, "w_out": D, "b_qkv": 3 * D, "b_ky": D, "b_proj": D,
           "w_gate": E * INNER, "w_up": E * INNER, "w_down": E * IC * D, "w_router": ROUTED,
           "router_bias": TT * ROUTED}


def build(nc, x_in, ins, out):
    ctx = ExitStack()
    with ctx:
        def sb(name, shape):
            return ctx.enter_context(nc.sbuf_tensor(name, shape, F32))

        def sem(name):
            return ctx.enter_context(nc.semaphore(name))

        psum = ctx.enter_context(nc.psum_tensor("psum", [128, 8, 512], F32))

        def bank(n, width=512):
            return psum[:, n, 0:width]

        x_res = sb("x_res", [128, (B + 1) * TT * D])
        const = {k: sb(k, [128, w]) for k, w in CONSTANTS.items()}
        w = {k: sb(k, [128, n]) for k, n in WEIGHTS.items()}
        ident = const["identity"]
        stats = sb("stats", [128, TT, 6])
        mean_var = sb("mean_var", [128, TT, 2])
        var_eps = sb("var_eps", [128, TT])
        neg_half = sb("neg_half", [128, TT])
        rstd = sb("rstd", [128, TT])
        x_hat = sb("x_hat", [128, TT, D])
        xT = sb("xT", [128, T])

        def xs(n, t=0, tiles=1):
            return x_res[:, bass.ds((n - 1) * (TT * D) + t * D, tiles * D)]

        starts = {engine: [] for engine in ("tensor", "vector", "scalar", "pool")}

        def signals(engine, prefix, **steps):
            made = [(sem(f"{prefix}_{name}"), k) for name, k in steps.items()]
            starts[engine] += made
            return [s for s, _ in made]

        def start(eng, engine):
            for s, k in starts[engine]:
                eng.sem_inc(s, k)

        work = sb("work", [128, 13 * T])
        big = sb("big", [128, 2 * H * T])
        values = sb("values", [128, TT, H, OW])
        kv_bd = sb("kv_bd", [128, D + H])
        oT = sb("oT", [128, T])
        o_tok = sb("o_tok", [128, TT, D])
        den = sb("den", [128, TT, H])
        rec = sb("rec", [128, TT, H])
        pick = sb("pick", [128, H, D])
        logit = sb("logit", [128, TT, ROUTED])
        route = sb("route", [128, 6, TT, ROUTED])
        best = sb("best", [128, 6, TT])
        gate_weight = sb("gate_weight", [128, TT, ROUTED])
        dram_eps = nc.dram_tensor("eps_rows", (H, T), F32, kind="Internal").ap()

        loaded_x0, loaded_x, loaded_first, loaded = (sem(k) for k in ("loaded_x0", "loaded_x", "loaded_first", "loaded"))
        setup = sem("setup")
        SETUP = 6 + 2 * TT
        first_loads = ["identity", "w_qkv", "w_qk_rot", "rope_q", "rope_k", "same_head", "w_out", "head_mask"]
        rest_loads = [k for k in [*const, *w] if k not in first_loads]

        class Norm:

            def __init__(self, name, used, used_count):
                self.used, self.used_count = used, used_count
                self.stats_done, self.mean_done, self.var_ready, self.hat_ready = signals(
                    "vector", name, stats_done=TT, mean_done=TT, var_ready=1, hat_ready=TT)
                self.rstd_ready, = signals("pool", name, rstd_ready=1)
                self.turned, = signals("tensor", name, turned=1)
                self.xT_ready, = signals("scalar", name, xT_ready=1)
                self.go = sem(f"{name}_go")

            def vector_stats(self, v, n):
                for t in range(TT):
                    nc.vector.bn_stats(stats[:, t, :], xs(n, t)).then_inc(self.stats_done, 1)
                v.wait_ge(self.stats_done, n * TT + TT)
                v.wait_ge(self.hat_ready, n * TT)
                v.sem_inc(self.go, 1)
                for t in range(TT):
                    nc.vector.bn_aggr(mean_var[:, t, :], stats[:, t, :]).then_inc(self.mean_done, 1)
                v.wait_ge(self.mean_done, n * TT + TT)
                nc.vector.tensor_scalar(var_eps[:], mean_var[:, :, 1], LN_EPS, None, ALU.add).then_inc(self.var_ready, 1)

            def pool_rstd(self, p, n):
                p.wait_ge(self.var_ready, n + 1)
                nc.gpsimd.tensor_tensor(rstd[:], var_eps[:], neg_half[:], ALU.pow).then_inc(self.rstd_ready, 1)

            def vector_hat(self, v, n):
                v.wait_ge(self.rstd_ready, n + 1)
                v.wait_ge(self.turned, n)
                for t in range(TT):
                    nc.vector.tensor_scalar(x_hat[:, t, :], xs(n, t), mean_var[:, t, 0:1], rstd[:, t:t + 1],
                                            ALU.subtract, ALU.mult).then_inc(self.hat_ready, 1)

            def tensor_turn(self, pe, n, to):
                pe.wait_ge(self.hat_ready, n * TT + TT)
                pe.wait_ge(self.xT_ready, n)
                for t in range(TT):
                    mm = nc.tensor.transpose(bank(to)[:, t * 128:(t + 1) * 128], x_hat[:, t, :], ident[:])
                mm.then_inc(self.turned, 1)

            def scalar_copy(self, a, n, frm):
                a.wait_ge(self.turned, n + 1)
                a.wait_ge(self.used, n * self.used_count)
                nc.scalar.copy(xT[:], bank(frm)).then_inc(self.xT_ready, 1)

        def num_den(first_bank):
            return psum[:, first_bank:first_bank + 2, :].rearrange("p b (t n) -> p (b t) n", t=2)

        def after(eng, previous):
            if previous:
                x_done, count, norm = previous
                eng.wait_ge(x_done, count)
                eng.wait_ge(norm.xT_ready, B + 2)

        a_q, a_kv, a_sum, a_num, a_oT, a_y = signals("tensor", "a", q=1, kv=1, sum=1, num=1, oT=1, y=1)
        a_prod, a_rope, a_min, a_feat, a_bd, a_den, a_rec, a_o, a_x = signals(
            "vector", "a", prod=4, rope=2, min=2, feat=2, bd=2, den=1, rec=1, o=1, x=1)
        a_exp, a_v, a_oTc = signals("scalar", "a", exp=2, v=1, oTc=1)
        na = Norm("a", a_kv, 1)
        q_prod = work[:, 0:2 * T].rearrange("p (a n) -> p a n", a=2)
        k_prod = work[:, 2 * T:4 * T].rearrange("p (a n) -> p a n", a=2)
        q_exp, k_exp = work[:, 4 * T:5 * T], work[:, 5 * T:6 * T]
        q_feat, k_feat = work[:, 6 * T:7 * T], work[:, 7 * T:8 * T]
        v_ones = big[:, 0:TT * (D + 1)].rearrange("p (t n) -> p t n", t=TT)
        rope_q = const["rope_q"][:].rearrange("p (a n) -> p a n", a=2)
        rope_k = const["rope_k"][:].rearrange("p (a n) -> p a n", a=2)
        tiles = lambda ap: ap.rearrange("p (t n) -> p t n", t=TT)

        def attn_a_tensor(pe):
            na.tensor_turn(pe, 1, 6)
            with pe.Fori(1, B + 1) as b:
                pe.wait_ge(na.xT_ready, b + 1)
                pe.wait_ge(a_o, b)
                nc.tensor.matmul(bank(0), w["w_qkv"][:, 0:D], xT[:], start=True, stop=True)
                nc.tensor.matmul(bank(1), w["w_qk_rot"][:, 0:D], xT[:], start=True, stop=True).then_inc(a_q, 1)
                pe.wait_ge(a_x, b)
                pe.wait_ge(a_v, b)
                pe.wait_ge(a_feat, 2 * b)
                for t in range(TT):
                    lhsT = xT[:, t * 128:(t + 1) * 128]
                    nc.tensor.matmul(bank(2 + t, 2 * D), lhsT, w["w_qkv"][:, D:3 * D], start=True, stop=True)
                    mm = nc.tensor.matmul(psum[:, 2 + t, 2 * D:3 * D], lhsT, w["w_qk_rot"][:, D:2 * D],
                                          start=True, stop=True)
                mm.then_inc(a_kv, 1)
                na.tensor_turn(pe, b + 1, 6)
                pe.wait_ge(a_feat, 2 * b + 2)
                pe.wait_ge(a_v, b + 1)
                pe.wait_ge(a_oTc, b)
                for t in range(TT):
                    mm = nc.tensor.matmul(bank(7, D + 1), tiles(k_feat)[:, t, :], v_ones[:, t, :],
                                          start=t == 0, stop=t == TT - 1)
                mm.then_inc(a_sum, 1)
                pe.wait_ge(a_bd, 2 * b + 2)
                for t in range(TT):
                    mm = nc.tensor.matmul(num_den(0)[:, t, 0:D + H], tiles(q_feat)[:, t, :], kv_bd[:],
                                          start=True, stop=True)
                mm.then_inc(a_num, 1)
                pe.wait_ge(a_o, b + 1)
                for t in range(TT):
                    mm = nc.tensor.transpose(tiles(bank(7))[:, t, :], o_tok[:, t, :], ident[:])
                mm.then_inc(a_oT, 1)
                pe.wait_ge(a_oTc, b + 1)
                for t in range(TT):
                    mm = nc.tensor.matmul(tiles(bank(2))[:, t, :], oT[:, t * 128:(t + 1) * 128], w["w_out"][:],
                                          start=True, stop=True)
                mm.then_inc(a_y, 1)

        def attn_a_vector(v):
            na.vector_stats(v, 1)
            na.vector_hat(v, 1)
            with v.Fori(1, B + 1) as b:
                v.wait_ge(a_q, b + 1)
                nc.vector.tensor_tensor(q_prod[:, 0, :], bank(0), rope_q[:, 0, :], ALU.mult).then_inc(a_prod, 1)
                nc.vector.tensor_tensor(q_prod[:, 1, :], bank(1), rope_q[:, 1, :], ALU.mult).then_inc(a_prod, 1)
                v.wait_ge(a_kv, b + 1)
                nc.vector.tensor_tensor(tiles(k_prod[:, 0, :]), psum[:, 2:2 + TT, 0:D], tiles(rope_k[:, 0, :]),
                                        ALU.mult).then_inc(a_prod, 1)
                nc.vector.tensor_tensor(tiles(k_prod[:, 1, :]), psum[:, 2:2 + TT, 2 * D:3 * D],
                                        tiles(rope_k[:, 1, :]), ALU.mult).then_inc(a_prod, 1)
                for n, prod in enumerate((q_prod, k_prod)):
                    v.wait_ge(a_prod, 4 * b + 2 * n + 2)
                    nc.vector.tensor_tensor(prod[:, 0, :], prod[:, 0, :], prod[:, 1, :], ALU.add).then_inc(a_rope, 1)
                for n, (prod, e) in enumerate(((q_prod, q_exp), (k_prod, k_exp))):
                    v.wait_ge(a_rope, 2 * b + n + 1)
                    nc.vector.tensor_scalar(e, prod[:, 0, :], 0.0, None, ALU.min).then_inc(a_min, 1)
                na.vector_stats(v, b + 1)
                for n, (prod, e, feat) in enumerate(((q_prod, q_exp, q_feat), (k_prod, k_exp, k_feat))):
                    v.wait_ge(a_exp, 2 * b + n + 1)
                    v.wait_ge((a_num, a_sum)[n], b)
                    nc.vector.scalar_tensor_tensor(feat, prod[:, 0, :], 0.0, e, ALU.max, ALU.add).then_inc(a_feat, 1)
                na.vector_hat(v, b + 1)
                v.wait_ge(a_sum, b + 1)
                nc.vector.tensor_tensor(kv_bd[:, 0:D], bank(7, D), const["same_head"][:], ALU.mult).then_inc(a_bd, 1)
                nc.vector.tensor_scalar(kv_bd[:, D:D + H], const["head_mask"][:], psum[:, 7, D:D + 1], None,
                                        ALU.mult).then_inc(a_bd, 1)
                v.wait_ge(a_num, b + 1)
                nc.vector.tensor_scalar(den[:], num_den(0)[:, :, D:D + H], EPS, None, ALU.max).then_inc(a_den, 1)
                v.wait_ge(a_den, b + 1)
                nc.vector.reciprocal(rec[:], den[:]).then_inc(a_rec, 1)
                v.wait_ge(a_rec, b + 1)
                v.wait_ge(a_oT, b)
                nc.vector.tensor_tensor(o_tok[:].rearrange("p t (h d) -> p t h d", d=HD),
                                        num_den(0)[:, :, 0:D].rearrange("p t (h d) -> p t h d", d=HD),
                                        rec[:].unsqueeze(3).broadcast_to([128, TT, H, HD]),
                                        ALU.mult).then_inc(a_o, 1)
                v.wait_ge(a_y, b + 1)
                nc.vector.tensor_tensor(xs(b, 0, TT), bank(2), xs(b, 0, TT), ALU.add).then_inc(a_x, 1)

        def attn_a_scalar(a):
            na.scalar_copy(a, 1, 6)
            with a.Fori(1, B + 1) as b:
                a.wait_ge(a_prod, 4 * b + 4)
                a.wait_ge(a_sum, b)
                nc.scalar.copy(v_ones[:, :, 0:D], psum[:, 2:2 + TT, D:2 * D]).then_inc(a_v, 1)
                for n, e in enumerate((q_exp, k_exp)):
                    a.wait_ge(a_min, 2 * b + n + 1)
                    nc.scalar.activation(e, e, ACT.Exp).then_inc(a_exp, 1)
                na.scalar_copy(a, b + 1, 6)
                a.wait_ge(a_oT, b + 1)
                a.wait_ge(a_y, b)
                nc.scalar.copy(oT[:], bank(7)).then_inc(a_oTc, 1)

        def attn_a_pool(p):
            na.pool_rstd(p, 1)
            with p.Fori(1, B + 1) as b:
                na.pool_rstd(p, b + 1)

        silu_out = work[:, 0:IC * T].rearrange("p (c n) -> p c n", c=IC)
        hidden = work[:, IC * T:3 * IC * T].rearrange("p (e c n) -> p e c n", e=2, c=IC)
        w_gate = w["w_gate"][:].rearrange("p (e c n) -> p e c n", e=E, c=IC)
        w_up = w["w_up"][:].rearrange("p (e c n) -> p e c n", e=E, c=IC)
        w_down = w["w_down"][:].rearrange("p (e c n) -> p e c n", e=E, c=IC)
        by_expert = lambda ap: ap.rearrange("p (t e) -> p t e", e=ROUTED)
        spread = lambda ap: ap.unsqueeze(2).broadcast_to([128, TT, ROUTED])
        EC = E * IC
        XC = 1 + ROUTED * TT
        LINKS = 17

        class Experts:
            def __init__(self, name, previous):
                self.previous = previous
                self.logits, self.gate_up, self.y = signals("tensor", name, logits=1, gate_up=EC, y=E)
                self.logit_ready, self.chain, self.weight_ready, self.hidden, self.x = signals(
                    "vector", name, logit_ready=1, chain=LINKS, weight_ready=1, hidden=EC, x=XC)
                self.exp_ready, self.silu = signals("scalar", name, exp_ready=1, silu=EC)
                self.norm = Norm(name, self.gate_up, EC)
                self.done = (self.x, (B + 1) * XC, self.norm)

            def tensor(self, pe):
                after(pe, self.previous)
                self.norm.tensor_turn(pe, 1, 6)
                with pe.Fori(1, B + 1) as b:
                    pe.wait_ge(self.norm.xT_ready, b + 1)
                    pe.wait_ge(self.logit_ready, b)
                    for t in range(TT):
                        mm = nc.tensor.matmul(psum[:, 7, t * ROUTED:(t + 1) * ROUTED], xT[:, t * 128:(t + 1) * 128],
                                              w["w_router"][:], start=True, stop=True)
                    mm.then_inc(self.logits, 1)
                    for e in range(E + 1):
                        if e < E:
                            for c in range(IC):
                                pe.wait_ge(self.hidden, b * EC + max(e * IC + c - 1, 0))
                                nc.tensor.matmul(bank(c), w_gate[:, e, c, :], xT[:], start=True, stop=True)
                                nc.tensor.matmul(bank(2 + c), w_up[:, e, c, :], xT[:], start=True,
                                                 stop=True).then_inc(self.gate_up, 1)
                        if e == E - 1:
                            self.norm.tensor_turn(pe, b + 1, 6)
                        if e > 0:
                            pe.wait_ge(self.hidden, b * EC + e * IC)
                            done = 0 if e < 3 else 1 + (e - 3) * TT
                            pe.wait_ge(self.x, b * XC + done)
                            for t in range(TT):
                                for c in range(IC):
                                    mm = nc.tensor.matmul(tiles(bank(4 + (e - 1) % 2))[:, t, :],
                                                          hidden[:, (e - 1) % 2, c, t * 128:(t + 1) * 128],
                                                          w_down[:, e - 1, c, :], start=c == 0, stop=c == IC - 1)
                            mm.then_inc(self.y, 1)

            def scalar(self, a):
                after(a, self.previous)
                self.norm.scalar_copy(a, 1, 6)
                with a.Fori(1, B + 1) as b:
                    a.wait_ge(self.logit_ready, b + 1)
                    nc.scalar.activation(route[:, 0], logit[:], ACT.Exp, scale=-1.0).then_inc(self.exp_ready, 1)
                    for e in range(E):
                        for c in range(IC):
                            a.wait_ge(self.gate_up, b * EC + e * IC + c + 1)
                            a.wait_ge(self.hidden, b * EC + max(e * IC + c - 1, 0))
                            nc.scalar.activation(silu_out[:, c, :], bank(c), ACT.Silu).then_inc(self.silu, 1)
                    self.norm.scalar_copy(a, b + 1, 6)

            def pool(self, p):
                after(p, self.previous)
                self.norm.pool_rstd(p, 1)
                with p.Fori(1, B + 1) as b:
                    self.norm.pool_rstd(p, b + 1)

            def routing(self, v, b):
                links = [0]

                def link(ins):
                    links[0] += 1
                    ins.then_inc(self.chain, 1)
                    v.wait_ge(self.chain, b * LINKS + links[0])

                v.wait_ge(self.logits, b + 1)
                v.wait_ge(self.exp_ready, b)
                nc.vector.tensor_tensor(logit[:], by_expert(bank(7, TT * ROUTED)), by_expert(w["router_bias"][:]),
                                        ALU.add).then_inc(self.logit_ready, 1)
                v.wait_ge(self.exp_ready, b + 1)
                prob, first, second, score = (route[:, k] for k in range(1, 5))
                left = route[:, 5]
                link(nc.vector.tensor_scalar(score, route[:, 0], 1.0, None, ALU.add))
                link(nc.vector.reciprocal(prob, score))
                link(nc.vector.tensor_reduce(best[:, 0], prob, AX.X, ALU.max))
                rank = by_expert(const["choice_rank"][:])
                for n, (p, chosen) in enumerate(((prob, first), (left, second))):
                    link(nc.vector.tensor_tensor(score, p, spread(best[:, 3 * n]), ALU.is_equal))
                    link(nc.vector.tensor_tensor(score, score, rank, ALU.mult))
                    link(nc.vector.tensor_reduce(best[:, 3 * n + 1], score, AX.X, ALU.max))
                    link(nc.vector.tensor_tensor(chosen, score, spread(best[:, 3 * n + 1]), ALU.is_equal))
                    if n == 0:
                        link(nc.vector.scalar_tensor_tensor(left, first, -2.0, prob, ALU.mult, ALU.add))
                        link(nc.vector.tensor_reduce(best[:, 3], left, AX.X, ALU.max))
                link(nc.vector.tensor_tensor(best[:, 2], best[:, 0], best[:, 3], ALU.add))
                link(nc.vector.reciprocal(best[:, 5], best[:, 2]))
                link(nc.vector.tensor_tensor(score, first, second, ALU.add))
                link(nc.vector.tensor_tensor(score, score, prob, ALU.mult))
                assert links[0] == LINKS, links
                nc.vector.tensor_tensor(gate_weight[:], score, spread(best[:, 5]), ALU.mult).then_inc(self.weight_ready, 1)

            def vector(self, v):
                after(v, self.previous)
                self.norm.vector_stats(v, 1)
                self.norm.vector_hat(v, 1)
                with v.Fori(1, B + 1) as b:
                    self.routing(v, b)
                    for e in range(E + 1):
                        if e < E:
                            for c in range(IC):
                                v.wait_ge(self.silu, b * EC + e * IC + c + 1)
                                if c == 0:
                                    v.wait_ge(self.y, b * E + max(e - 1, 0))
                                nc.vector.tensor_tensor(hidden[:, e % 2, c, :], bank(2 + c), silu_out[:, c, :],
                                                        ALU.mult).then_inc(self.hidden, 1)
                        if e == 4:
                            self.norm.vector_stats(v, b + 1)
                        if e == 6:
                            self.norm.vector_hat(v, b + 1)
                        if e > 0:
                            v.wait_ge(self.y, b * E + e)
                            y = tiles(bank(4 + (e - 1) % 2))
                            if e == 1:
                                nc.vector.tensor_tensor(xs(b, 0, TT), bank(4), xs(b, 0, TT), ALU.add).then_inc(self.x, 1)
                                v.wait_ge(self.weight_ready, b + 1)
                                continue
                            v.wait_ge(self.x, b * XC + 1 + (e - 2) * TT)
                            for t in range(TT):
                                nc.vector.scalar_tensor_tensor(xs(b, t), y[:, t, :], gate_weight[:, t, e - 2:e - 1],
                                                               xs(b, t), ALU.mult, ALU.add).then_inc(self.x, 1)

        UNITS = [(k, k) for k in range(TT)] + [(k, q) for k in range(TT) for q in range(k + 1, TT)]
        STEPS = [(g, 2 * s, UNITS[2 * s:2 * s + 2]) for g in range(GROUPS) for s in range(len(UNITS) // 2)]
        NS = len(STEPS)
        masked = [i for i, (_, u, _) in enumerate(STEPS) if u < TT]
        NM = len(masked)
        RING = 4
        head_q = big[:, 0:H * T].rearrange("p (h n) -> p h n", h=H)
        eps_row = big[:, H * T:2 * H * T].rearrange("p (h n) -> p h n", h=H)
        b_qT, b_kT, b_kyT, b_rT, b_eT = (work[:, n * T:(n + 1) * T] for n in range(5))
        ring = work[:, 5 * T:(5 + 2 * RING) * T].rearrange("p (r n) -> p r n", r=RING)
        half_sums = sb("half_sums", [OW, 2, T])

        class LogAttention:
            def __init__(self, previous):
                self.previous = previous
                (self.proj, self.score, self.sum_a, self.score_b, self.sum_b, self.num, self.oT, self.y) = signals(
                    "tensor", "b", proj=1, score=NS, sum_a=NS, score_b=NS, sum_b=NS, num=1, oT=1, y=1)
                (self.v_ready, self.head_q, self.clip, self.sum_eps, self.recip, self.eps_ready, self.head_r,
                 self.ratio, self.den, self.rec, self.o, self.x) = signals(
                    "vector", "b", v_ready=TT, head_q=H, clip=NS, sum_eps=1, recip=1, eps_ready=1, head_r=H,
                    ratio=NS, den=1, rec=1, o=2, x=1)
                (self.q_ready, self.k_ready, self.exp, self.abs, self.ln, self.half_ready, self.oTc) = signals(
                    "scalar", "b", q_ready=1, k_ready=2, exp=NS, abs=NS, ln=NS, half_ready=2, oTc=1)
                self.mask_a, self.mask_b = signals("pool", "b", mask_a=NM, mask_b=NM)
                self.stored, self.spread = sem("b_stored"), sem("b_spread")
                self.norm = Norm("b", self.proj, 1)
                self.go, self.sync_go = sem("b_mask_go"), sem("b_sync_go")
                self.done = (self.x, B + 1, self.norm)

            def products(self, pe, b, i, kT, score, evacuated):
                g, _, units = STEPS[i]
                pe.wait_ge(evacuated, b * NS + max(i - 1, 0))
                for n, (kb, qb) in enumerate(units):
                    mm = nc.tensor.matmul(bank(2 * (i % 2) + n), kT[:, kb * 128:(kb + 1) * 128],
                                          head_q[:, 4 * g:4 * g + 4, qb * 128:(qb + 1) * 128], start=True, stop=True)
                mm.then_inc(score, 1)

            def tensor(self, pe):
                after(pe, self.previous)
                self.norm.tensor_turn(pe, 1, 7)
                with pe.Fori(1, B + 1) as b:
                    pe.wait_ge(self.norm.xT_ready, b + 1)
                    pe.wait_ge(self.x, b)
                    nc.tensor.matmul(bank(4), w["b_qkv"][:, 0:D], xT[:], start=True, stop=True)
                    nc.tensor.matmul(bank(5), w["b_ky"][:], xT[:], start=True, stop=True)
                    nc.tensor.matmul(bank(6), w["b_qkv"][:, D:2 * D], xT[:], start=True, stop=True)
                    for t in range(TT):
                        mm = nc.tensor.matmul(tiles(bank(7))[:, t, :], xT[:, t * 128:(t + 1) * 128],
                                              w["b_qkv"][:, 2 * D:3 * D], start=True, stop=True)
                    mm.then_inc(self.proj, 1)
                    pe.wait_ge(self.k_ready, 2 * b + 2)
                    for i in range(NS + 2):
                        if i < NS:
                            g, s, _ = STEPS[i]
                            if s == 0:
                                pe.wait_ge(self.head_q, b * H + 4 * g + 4)
                            self.products(pe, b, i, b_kyT, self.score, self.exp)
                        if i >= 2:
                            j = i - 2
                            g, _, units = STEPS[j]
                            pe.wait_ge(self.clip, b * NS + j + 1)
                            if j in masked:
                                pe.wait_ge(self.mask_a, b * NM + masked.index(j) + 1)
                            for n, (kb, qb) in enumerate(units):
                                for h in range(4):
                                    mm = nc.tensor.matmul(bank(4)[:, qb * 128:(qb + 1) * 128], pick[:, 4 * g + h, :],
                                                          ring[:, j % RING, n * T + h * 128:n * T + (h + 1) * 128],
                                                          start=j == 0 and n == 0 and h == 0,
                                                          stop=j == NS - 1 and n == 1 and h == 3, skip_group_check=True)
                            mm.then_inc(self.sum_a, 1)
                    pe.wait_ge(self.v_ready, (b + 1) * TT)
                    self.norm.tensor_turn(pe, b + 1, 7)
                    for i in range(NS + 2):
                        if i < NS:
                            g, s, _ = STEPS[i]
                            if s == 0:
                                pe.wait_ge(self.head_r, b * H + 4 * g + 4)
                            if i < 2:
                                pe.wait_ge(self.exp, (b + 1) * NS)
                            self.products(pe, b, i, b_kT, self.score_b, self.abs)
                        if i >= 2:
                            j = i - 2
                            g, _, units = STEPS[j]
                            pe.wait_ge(self.ln, b * NS + j + 1)
                            if j in masked:
                                pe.wait_ge(self.mask_b, b * NM + masked.index(j) + 1)
                            first, last = j % (NS // 2) == 0, j % (NS // 2) == NS // 2 - 1
                            for n, (kb, qb) in enumerate(units):
                                for h in range(4):
                                    mm = nc.tensor.matmul(psum[0:OW, 5 + g // 2, qb * 128:(qb + 1) * 128],
                                                          values[:, kb, 4 * g + h, :],
                                                          ring[:, j % RING, n * T + h * 128:n * T + (h + 1) * 128],
                                                          start=first and n == 0 and h == 0,
                                                          stop=last and n == 1 and h == 3, skip_group_check=True)
                            mm.then_inc(self.sum_b, 1)
                    pe.wait_ge(self.half_ready, 2 * b + 2)
                    for t in range(TT):
                        for half in range(2):
                            mm = nc.tensor.transpose(num_den(5)[:, t, half * OW:(half + 1) * OW],
                                                     half_sums[:, half, t * 128:(t + 1) * 128], ident[0:OW, 0:OW])
                    mm.then_inc(self.num, 1)
                    pe.wait_ge(self.o, 2 * b + 2)
                    pe.wait_ge(self.norm.xT_ready, b + 2)
                    for t in range(TT):
                        mm = nc.tensor.transpose(tiles(bank(7))[:, t, :], o_tok[:, t, :], ident[:])
                    mm.then_inc(self.oT, 1)
                    pe.wait_ge(self.oTc, b + 1)
                    pe.wait_ge(self.sum_eps, b + 1)
                    for t in range(TT):
                        mm = nc.tensor.matmul(tiles(bank(4))[:, t, :], oT[:, t * 128:(t + 1) * 128], w["b_proj"][:],
                                              start=True, stop=True)
                    mm.then_inc(self.y, 1)

            def scalar(self, a):
                after(a, self.previous)
                self.norm.scalar_copy(a, 1, 7)
                with a.Fori(1, B + 1) as b:
                    a.wait_ge(self.proj, b + 1)
                    a.wait_ge(self.head_r, b * H)
                    nc.scalar.copy(b_qT, bank(4)).then_inc(self.q_ready, 1)
                    a.wait_ge(self.score_b, b * NS)
                    nc.scalar.copy(b_kyT, bank(5)).then_inc(self.k_ready, 1)
                    nc.scalar.copy(b_kT, bank(6)).then_inc(self.k_ready, 1)
                    for i in range(NS):
                        a.wait_ge(self.score, b * NS + i + 1)
                        if i < RING:
                            a.wait_ge(self.sum_b, b * NS)
                        else:
                            a.wait_ge(self.sum_a, b * NS + i - RING + 1)
                        nc.scalar.activation(ring[:, i % RING, :], psum[:, 2 * (i % 2):2 * (i % 2) + 2, :],
                                             ACT.Exp).then_inc(self.exp, 1)
                    self.norm.scalar_copy(a, b + 1, 7)
                    for i in range(NS + 1):
                        if i < NS:
                            a.wait_ge(self.score_b, b * NS + i + 1)
                            if i < RING:
                                a.wait_ge(self.sum_a, (b + 1) * NS)
                            else:
                                a.wait_ge(self.sum_b, b * NS + i - RING + 1)
                            nc.scalar.activation(ring[:, i % RING, :], psum[:, 2 * (i % 2):2 * (i % 2) + 2, :],
                                                 ACT.Abs).then_inc(self.abs, 1)
                        if i > 0:
                            a.wait_ge(self.ratio, b * NS + i)
                            r = ring[:, (i - 1) % RING, :]
                            nc.scalar.activation(r, r, ACT.Ln, bias=1.0).then_inc(self.ln, 1)
                    a.wait_ge(self.sum_b, (b + 1) * NS)
                    a.wait_ge(self.num, b)
                    for half in range(2):
                        nc.scalar.copy(half_sums[:, half, :], psum[0:OW, 5 + half, :]).then_inc(self.half_ready, 1)
                    a.wait_ge(self.oT, b + 1)
                    a.wait_ge(self.y, b)
                    nc.scalar.copy(oT[:], bank(7)).then_inc(self.oTc, 1)

            def vector(self, v):
                after(v, self.previous)
                self.norm.vector_stats(v, 1)
                self.norm.vector_hat(v, 1)
                with v.Fori(1, B + 1) as b:
                    v.wait_ge(self.q_ready, b + 1)
                    v.wait_ge(self.score_b, b * NS)
                    for h in range(H):
                        nc.vector.tensor_scalar(head_q[:, h, :], b_qT, const["head_scale"][:, h:h + 1], None,
                                                ALU.mult).then_inc(self.head_q, 1)
                    v.wait_ge(self.proj, b + 1)
                    v.wait_ge(self.sum_b, b * NS)
                    for t in range(TT):
                        for half in range(2):
                            dst = values[:, t, half * HALF:(half + 1) * HALF, :].rearrange("p h n -> p (h n)")
                            dst = diagonal(dst)
                            ins = nc.vector.tensor_copy(dst, psum[:, 7, t * D + half * HALF * HD:
                                                                  t * D + (half + 1) * HALF * HD]
                                                        .rearrange("p (h d) -> p h d", d=HD))
                        ins.then_inc(self.v_ready, 1)
                    for i in range(NS):
                        v.wait_ge(self.exp, b * NS + i + 1)
                        nc.vector.tensor_scalar(ring[:, i % RING, :], ring[:, i % RING, :], CLIP_HI, CLIP_LO,
                                                ALU.min, ALU.max).then_inc(self.clip, 1)
                    self.norm.vector_stats(v, b + 1)
                    self.norm.vector_hat(v, b + 1)
                    v.wait_ge(self.sum_a, (b + 1) * NS)
                    nc.vector.tensor_scalar(b_rT, bank(4), EPS, None, ALU.add).then_inc(self.sum_eps, 1)
                    v.wait_ge(self.sum_eps, b + 1)
                    nc.vector.reciprocal(b_rT, b_rT).then_inc(self.recip, 1)
                    v.wait_ge(self.recip, b + 1)
                    nc.vector.tensor_scalar(b_eT, b_rT, EPS, None, ALU.mult).then_inc(self.eps_ready, 1)
                    for h in range(H):
                        nc.vector.scalar_tensor_tensor(head_q[:, h, :], b_qT, const["head_scale"][:, h:h + 1], b_rT,
                                                       ALU.mult, ALU.mult).then_inc(self.head_r, 1)
                    for i in range(NS):
                        g, _, units = STEPS[i]
                        v.wait_ge(self.abs, b * NS + i + 1)
                        v.wait_ge(self.spread, 16 * GROUPS * b)
                        for n, (kb, qb) in enumerate(units):
                            r = ring[:, i % RING, n * T:(n + 1) * T].rearrange("p (h n) -> p h n", h=4)
                            ins = nc.vector.tensor_tensor(r, r, eps_row[:, 4 * g:4 * g + 4, qb * 128:(qb + 1) * 128],
                                                          ALU.add)
                        ins.then_inc(self.ratio, 1)
                    v.wait_ge(self.num, b + 1)
                    halves = num_den(5)[:, :, 0:OT].rearrange("p t (a n) -> p t a n", a=2)
                    nc.vector.tensor_scalar(den[:].rearrange("p t (a h) -> p t a h", a=2),
                                            halves[:, :, :, HALF * HD:OW], EPS, None, ALU.add).then_inc(self.den, 1)
                    v.wait_ge(self.den, b + 1)
                    nc.vector.reciprocal(rec[:], den[:]).then_inc(self.rec, 1)
                    v.wait_ge(self.rec, b + 1)
                    v.wait_ge(self.oT, b)
                    for half in range(2):
                        lo, hi = half * HALF, (half + 1) * HALF
                        nc.vector.tensor_tensor(
                            o_tok[:, :, lo * HD:hi * HD].rearrange("p t (h d) -> p t h d", d=HD),
                            halves[:, :, half, 0:HALF * HD].rearrange("p t (h d) -> p t h d", d=HD),
                            rec[:, :, lo:hi].unsqueeze(3).broadcast_to([128, TT, HALF, HD]),
                            ALU.mult).then_inc(self.o, 1)
                    v.wait_ge(self.y, b + 1)
                    nc.vector.tensor_tensor(xs(b, 0, TT), bank(4), xs(b, 0, TT), ALU.add).then_inc(self.x, 1)

            def pool(self, p):
                after(p, self.previous)
                self.norm.pool_rstd(p, 1)
                with p.Fori(1, B + 1) as b:
                    for n, (ready, done) in enumerate(((self.clip, self.mask_a), (self.ln, self.mask_b))):
                        if n == 1:
                            self.norm.pool_rstd(p, b + 1)
                        for i in masked:
                            p.wait_ge(ready, b * NS + i + 1)
                            p.sem_inc(self.go, 1)
                            r = ring[:, i % RING, :].rearrange("p (u n) -> p u n", n=128)
                            nc.gpsimd.affine_select(out=r, in_=r, pattern=[[0, 8], [1, 128]], compare_op=ALU.is_ge,
                                                    fill=0.0, base=0, channel_multiplier=-1).then_inc(done, 1)

            def sync(self, s):
                after(s, self.previous)
                with s.Fori(1, B + 1) as b:
                    s.wait_ge(self.ratio, b * NS)
                    s.sem_inc(self.sync_go, 1)
                    s.wait_ge(self.eps_ready, b + 1)
                    s.dma_start(dram_eps, b_eT[0:128:HD, :]).then_inc(self.stored, 16)
                    s.wait_ge(self.stored, 16 * b)
                    for g in range(GROUPS):
                        s.dma_start(eps_row[:, 4 * g:4 * g + 4, :],
                                    dram_eps[4 * g:4 * g + 4, :].unsqueeze(0).broadcast_to([128, 4, T])
                                    ).then_inc(self.spread, 16)

        def diagonal(ap):
            return bass.AP(ap.tensor, ap.offset, [ap.ap[0], [OW + HD, HALF], [1, HD]])

        ffn_1 = Experts("f1", (a_x, B + 1, na))
        log_attn = LogAttention(ffn_1.done)
        ffn_2 = Experts("f2", log_attn.done)
        stored, store_go = sem("stored"), sem("store_go")

        block = ctx.enter_context(nc.Block())

        @block.sync
        def _(s):
            def load(name, signal):
                dst = const[name] if name in const else w[name]
                s.dma_start(dst[:], ins[name]).then_inc(signal, 16)

            for n in range(B):
                if n == 1:
                    for name in first_loads:
                        load(name, loaded_first)
                s.dma_start(tiles(x_res[:, n * TT * D:(n + 1) * TT * D]),
                            x_in[n * T:(n + 1) * T, :].rearrange("(t p) d -> p t d", p=128)
                            ).then_inc(loaded_x0 if n == 0 else loaded_x, 16)
            for name in rest_loads:
                load(name, loaded)
            log_attn.sync(s)
            after(s, log_attn.done)
            with s.Fori(1, B + 1) as b:
                target = out[bass.ds((b - 1) * T, T), :].rearrange("(t p) d -> p t d", p=128)
                source = tiles(xs(b, 0, TT))
                s.wait_ge(ffn_2.x, (b + 1) * XC)
                s.sem_inc(store_go, 1)
                s.dma_start(target, source).then_inc(stored, 16)
            s.wait_ge(stored, 16 * B)

        @block.gpsimd
        def _(p):
            start(p, "pool")
            nc.gpsimd.memset(neg_half[:], -0.5).then_inc(setup, 1)
            nc.gpsimd.memset(x_res[:, B * TT * D:], 0.0).then_inc(setup, 1)
            nc.gpsimd.memset(v_ones[:, :, D:D + 1], 1.0).then_inc(setup, 1)
            nc.gpsimd.memset(values[:], 0.0).then_inc(setup, 1)
            nc.gpsimd.memset(pick[:], 0.0).then_inc(setup, 1)
            p.wait_ge(setup, 5)
            for half in range(2):
                for t in range(TT):
                    block_of = values[:, t, half * HALF:(half + 1) * HALF, :].rearrange("p h n -> p (h n)")
                    nc.gpsimd.memset(bass.AP(block_of.tensor, block_of.offset + HALF * HD,
                                             [block_of.ap[0], [OW + 1, HALF], [1, 1]]), 1.0).then_inc(setup, 1)
            whole = pick[:].rearrange("p h n -> p (h n)")
            nc.gpsimd.memset(bass.AP(whole.tensor, whole.offset, [whole.ap[0], [D + HD, H], [1, HD]]),
                             1.0).then_inc(setup, 1)
            attn_a_pool(p)
            ffn_1.pool(p)
            log_attn.pool(p)
            ffn_2.pool(p)

        @block.vector
        def _(v):
            start(v, "vector")
            v.wait_ge(setup, SETUP)
            v.wait_ge(loaded_x0, 16)
            v.wait_ge(loaded_first, 16 * len(first_loads))
            v.wait_ge(loaded_x, 16 * (B - 1))
            attn_a_vector(v)
            v.wait_ge(loaded, 16 * len(rest_loads))
            ffn_1.vector(v)
            log_attn.vector(v)
            ffn_2.vector(v)

        @block.scalar
        def _(a):
            start(a, "scalar")
            a.wait_ge(setup, SETUP)
            attn_a_scalar(a)
            ffn_1.scalar(a)
            log_attn.scalar(a)
            ffn_2.scalar(a)

        @block.tensor
        def _(pe):
            start(pe, "tensor")
            pe.wait_ge(setup, SETUP)
            pe.wait_ge(loaded_first, 16 * len(first_loads))
            attn_a_tensor(pe)
            pe.wait_ge(loaded, 16 * len(rest_loads))
            ffn_1.tensor(pe)
            log_attn.tensor(pe)
            ffn_2.tensor(pe)


def lay_out(inputs):
    w_qkv = inputs["L0_attn_a_W_qkv"]
    turned = np.arange(D).reshape(H, 2, HD // 2)[:, ::-1].reshape(-1)

    def with_shared(shared, routed):
        return np.concatenate([shared[None], routed], 0)

    gate = with_shared(inputs["L0_ffn_sg_w"], inputs["L0_ffn_wg"])
    up = with_shared(inputs["L0_ffn_su_w"], inputs["L0_ffn_wu"])
    down = with_shared(inputs["L0_ffn_sd_w"], inputs["L0_ffn_wd"])
    laid = {
        "w_qkv": w_qkv,
        "w_qk_rot": np.concatenate([w_qkv[:, :D][:, turned], w_qkv[:, D:2 * D][:, turned]], 1),
        "w_out": inputs["L0_attn_a_W_out"],
        "b_qkv": inputs["L0_attn_b_w_qkv"].T,
        "b_ky": inputs["L0_attn_b_w_ky"].T,
        "b_proj": inputs["L0_attn_b_w_proj"].T,
        "w_gate": gate.transpose(2, 0, 1).reshape(D, -1),
        "w_up": up.transpose(2, 0, 1).reshape(D, -1),
        "w_down": down.reshape(E, D, IC, 128).transpose(3, 0, 2, 1).reshape(128, -1),
        "w_router": inputs["L0_ffn_router_w"].T,
        "router_bias": np.tile(inputs["L0_ffn_routing_bias"], (128, TT)),
    }
    return {k: np.ascontiguousarray(v) for k, v in laid.items()}


def kernel(**inputs):
    from concourse import bacc
    from concourse.bass_utils import run_bass_kernel_spmd

    inputs = {k: np.asarray(v) for k, v in inputs.items()}
    arrays = {"x": np.ascontiguousarray(inputs["L0_attn_a_x"].reshape(B * T, D)), **shape_constants(), **lay_out(inputs)}
    nc = bacc.Bacc("TRN2", target_bir_lowering=False, num_devices=1)
    dram = {k: nc.dram_tensor(f"in_{k}", a.shape, mybir.dt.from_np(a.dtype), kind="ExternalInput").ap()
            for k, a in arrays.items()}
    out = nc.dram_tensor("out", (B * T, D), F32, kind="ExternalOutput").ap()
    build(nc, dram["x"], dram, out)
    result = run_bass_kernel_spmd(nc, [{f"in_{k}": a for k, a in arrays.items()}], core_ids=[0])
    return result.results[0]["out"].reshape(B, T, D)
```

```python
from contextlib import ExitStack

import numpy as np

import concourse.bass as bass
from concourse import mybir

F32 = mybir.dt.float32
F32R = mybir.dt.float32r
ALU = mybir.AluOpType
ACT = mybir.ActivationFunctionType
AX = mybir.AxisListType

B, T, D = 8, 512, 128
H, HD = 16, 8
TT = T // 128
E, INNER = 9, 256
IC = INNER // 128
ROUTED = E - 1
SCALE = HD ** -0.5
LN_EPS = 1e-5
EPS = 1e-6
CLIP_LO, CLIP_HI = float(np.exp(np.float32(-15.0))), float(np.exp(np.float32(15.0)))
ROPE_BASE = 500000.0
GROUPS = H // 4
PARTS = 4
HALF = H // 2
OW = HALF * HD + HALF
OT = 2 * OW


def shape_constants():
    inv_freq = (1.0 / ROPE_BASE ** (np.arange(0, HD, 2, dtype=np.float32) / HD)).astype(np.float32)
    freqs = np.arange(T, dtype=np.float32)[:, None] * inv_freq[None, :]
    emb = np.concatenate([freqs, freqs], axis=-1).astype(np.float32)
    sign = np.where(np.arange(HD) < HD // 2, -1.0, 1.0).astype(np.float32)
    cos = np.tile(np.cos(emb), (1, H)).astype(np.float32)
    sin = np.tile(np.sin(emb) * sign, (1, H)).astype(np.float32)
    tables = {
        "rope_q": np.stack([cos.T * np.float32(SCALE), sin.T * np.float32(SCALE)], 1),
        "rope_k": np.stack([cos.reshape(TT, 128, D), sin.reshape(TT, 128, D)], 0)
        .transpose(2, 0, 1, 3),
        "identity": np.eye(128, dtype=np.float32),
    }
    head_of = np.arange(D) // HD
    tables["same_head"] = (head_of[:, None] == head_of[None, :]).astype(np.float32)
    tables["head_mask"] = (head_of[:, None] == np.arange(H)[None, :]).astype(np.float32)
    rows = np.array([[0, 0], [1, 0], [0, 1], [1, 1]], dtype=np.float32)
    tables["minus_low"] = np.tile(np.repeat(-rows, HD, axis=0), (4, 1))
    tables["choice_rank"] = np.tile(np.arange(ROUTED, 0, -1, dtype=np.float32), (128, TT))
    return {k: np.ascontiguousarray(v, dtype=np.float32).reshape(v.shape[0], -1) for k, v in tables.items()}


CONSTANTS = {"rope_q": 2 * T, "rope_k": 2 * TT * D, "identity": 128, "same_head": D, "head_mask": H,
             "minus_low": 2,
             "choice_rank": TT * ROUTED}
WEIGHTS = {"w_qk_rot": 2 * D, "w_qkv": 3 * D, "w_out": D, "b_q": GROUPS * 128, "b_ky": GROUPS * 128,
           "b_k": GROUPS * 128, "b_v": D, "b_proj": D,
           "w_gate": E * INNER, "w_up": E * INNER, "w_down": E * IC * D, "w_router": ROUTED,
           "router_bias": TT * ROUTED}


def build(nc, x_in, ins, out):
    ctx = ExitStack()
    with ctx:
        def sb(name, shape, dtype=F32):
            return ctx.enter_context(nc.sbuf_tensor(name, shape, dtype))

        def sem(name):
            return ctx.enter_context(nc.semaphore(name))

        psum = ctx.enter_context(nc.psum_tensor("psum", [128, 8, 512], F32))

        def bank(n, width=512):
            return psum[:, n, 0:width]

        x_res = sb("x_res", [128, (B + 1) * TT * D])
        const = {k: sb(k, [128, w]) for k, w in CONSTANTS.items() if not k.startswith("rope")}
        w = {k: sb(k, [128, n]) for k, n in WEIGHTS.items()}
        ident = const["identity"]
        stats = sb("stats", [128, TT, 6])
        mean_var = sb("mean_var", [128, TT, 2])
        var_eps = sb("var_eps", [128, TT])
        neg_half = sb("neg_half", [128, TT])
        rstd = sb("rstd", [128, TT])
        x_hat = sb("x_hat", [128, TT, D])
        xT = sb("xT", [128, T])

        def xs(n, t=0, tiles=1):
            return x_res[:, bass.ds((n - 1) * (TT * D) + t * D, tiles * D)]

        starts = {engine: [] for engine in ("tensor", "vector", "scalar", "pool")}

        def signals(engine, prefix, passed=1.0, **steps):
            made = [(sem(f"{prefix}_{name}"), k) for name, k in steps.items()]
            starts[engine] += [(s, int(k * passed)) for s, k in made if passed]
            return [s for s, _ in made]

        def start(eng, engine):
            for s, k in starts[engine]:
                eng.sem_inc(s, k)

        stacks = sb("stacks", [128, (H + 2 + GROUPS) * T], F32R)
        x_high, x_low = (sb(k, [128, T], F32R)[:] for k in ("x_high", "x_low"))
        ring_a = sb("ring_a", [128, 8 * T])
        ring_b = sb("ring_b", [128, 8 * T])
        r_rows = sb("r_rows", [128, 2, GROUPS * T])
        values = sb("values", [128, TT, H, OW])
        kv_bd = sb("kv_bd", [128, D + H])
        oT = sb("oT", [128, T])
        o_tok = sb("o_tok", [128, TT, D])
        den = sb("den", [128, TT, H])
        rec = sb("rec", [128, TT, H])
        logit = sb("logit", [128, TT, ROUTED])
        route = sb("route", [128, 6, TT, ROUTED])
        best = sb("best", [128, 6, TT])
        gate_weight = sb("gate_weight", [128, TT, ROUTED])
        dram_r = nc.dram_tensor("r_scratch", (H, 128), F32, kind="Internal").ap()

        loaded_x0, loaded_x, loaded_first, loaded = (sem(k) for k in ("loaded_x0", "loaded_x", "loaded_first", "loaded"))
        setup = sem("setup")
        SETUP = 4 + 2 * TT
        first_loads = ["identity", "w_qkv", "w_qk_rot", "rope_q", "rope_k", "same_head", "w_out", "head_mask"]
        rest_loads = [k for k in [*const, *w] if k not in first_loads]

        class Norm:

            def __init__(self, name, used, used_count, used_before=0):
                self.used, self.used_count, self.used_before = used, used_count, used_before
                self.stats_done, self.mean_done, self.var_ready, self.hat_ready = signals(
                    "vector", name, stats_done=TT, mean_done=TT, var_ready=1, hat_ready=TT)
                self.rstd_ready, = signals("pool", name, rstd_ready=1)
                self.turned, = signals("tensor", name, turned=1)
                self.xT_ready, = signals("scalar", name, xT_ready=1)
                self.go = sem(f"{name}_go")

            def vector_stats(self, v, n):
                for t in range(TT):
                    nc.vector.bn_stats(stats[:, t, :], xs(n, t)).then_inc(self.stats_done, 1)
                v.wait_ge(self.stats_done, n * TT + TT)
                v.wait_ge(self.hat_ready, n * TT)
                v.sem_inc(self.go, 1)
                for t in range(TT):
                    nc.vector.bn_aggr(mean_var[:, t, :], stats[:, t, :]).then_inc(self.mean_done, 1)
                v.wait_ge(self.mean_done, n * TT + TT)
                nc.vector.tensor_scalar(var_eps[:], mean_var[:, :, 1], LN_EPS, None, ALU.add).then_inc(self.var_ready, 1)

            def pool_rstd(self, p, n):
                p.wait_ge(self.var_ready, n + 1)
                nc.gpsimd.tensor_tensor(rstd[:], var_eps[:], neg_half[:], ALU.pow).then_inc(self.rstd_ready, 1)

            def vector_hat(self, v, n):
                v.wait_ge(self.rstd_ready, n + 1)
                v.wait_ge(self.turned, n)
                for t in range(TT):
                    nc.vector.tensor_scalar(x_hat[:, t, :], xs(n, t), mean_var[:, t, 0:1], rstd[:, t:t + 1],
                                            ALU.subtract, ALU.mult).then_inc(self.hat_ready, 1)

            def tensor_turn(self, pe, n, to):
                pe.wait_ge(self.hat_ready, n * TT + TT)
                pe.wait_ge(self.xT_ready, n)
                for t in range(TT):
                    mm = nc.tensor.transpose(bank(to)[:, t * 128:(t + 1) * 128], x_hat[:, t, :], ident[:])
                mm.then_inc(self.turned, 1)

            def scalar_copy(self, a, n, frm):
                a.wait_ge(self.turned, n + 1)
                a.wait_ge(self.used, n * self.used_count - self.used_before)
                nc.scalar.copy(xT[:], bank(frm)).then_inc(self.xT_ready, 1)

        def num_den(first_bank):
            return psum[:, first_bank:first_bank + 2, :].rearrange("p b (t n) -> p (b t) n", t=2)

        def after(eng, previous):
            if previous:
                x_done, count, norm = previous
                eng.wait_ge(x_done, count)
                eng.wait_ge(norm.xT_ready, B + 2)

        a_q, a_kv, a_sum, a_num, a_oT, a_y = signals("tensor", "a", q=1, kv=1, sum=1, num=1, oT=1, y=1)
        a_prod, a_rope, a_min, a_feat, a_bd, a_den, a_rec, a_o, a_x = signals(
            "vector", "a", prod=4, rope=2, min=2, feat=2, bd=2, den=1, rec=1, o=1, x=1)
        a_exp, a_v, a_oTc = signals("scalar", "a", exp=2, v=1, oTc=1)
        na = Norm("a", a_kv, 1)
        q_prod = ring_a[:, 0:2 * T].rearrange("p (a n) -> p a n", a=2)
        k_prod = ring_a[:, 2 * T:4 * T].rearrange("p (a n) -> p a n", a=2)
        q_exp, k_exp = ring_a[:, 4 * T:5 * T], ring_a[:, 5 * T:6 * T]
        q_feat, k_feat = ring_a[:, 6 * T:7 * T], ring_a[:, 7 * T:8 * T]
        v_ones = r_rows[:, 0, 0:TT * (D + 1)].rearrange("p (t n) -> p t n", t=TT)
        rope_q = ring_b[:, 0:2 * T].rearrange("p (a n) -> p a n", a=2)
        rope_k = ring_b[:, 2 * T:2 * T + 2 * TT * D].rearrange("p (a n) -> p a n", a=2)
        tiles = lambda ap: ap.rearrange("p (t n) -> p t n", t=TT)

        def attn_a_tensor(pe):
            na.tensor_turn(pe, 1, 6)
            with pe.Fori(1, B + 1) as b:
                pe.wait_ge(na.xT_ready, b + 1)
                pe.wait_ge(a_o, b)
                nc.tensor.matmul(bank(0), w["w_qkv"][:, 0:D], xT[:], start=True, stop=True)
                nc.tensor.matmul(bank(1), w["w_qk_rot"][:, 0:D], xT[:], start=True, stop=True).then_inc(a_q, 1)
                pe.wait_ge(a_x, b)
                pe.wait_ge(a_v, b)
                pe.wait_ge(a_feat, 2 * b)
                for t in range(TT):
                    lhsT = xT[:, t * 128:(t + 1) * 128]
                    nc.tensor.matmul(bank(2 + t, 2 * D), lhsT, w["w_qkv"][:, D:3 * D], start=True, stop=True)
                    mm = nc.tensor.matmul(psum[:, 2 + t, 2 * D:3 * D], lhsT, w["w_qk_rot"][:, D:2 * D],
                                          start=True, stop=True)
                mm.then_inc(a_kv, 1)
                na.tensor_turn(pe, b + 1, 6)
                pe.wait_ge(a_feat, 2 * b + 2)
                pe.wait_ge(a_v, b + 1)
                pe.wait_ge(a_oTc, b)
                for t in range(TT):
                    mm = nc.tensor.matmul(bank(7, D + 1), tiles(k_feat)[:, t, :], v_ones[:, t, :],
                                          start=t == 0, stop=t == TT - 1)
                mm.then_inc(a_sum, 1)
                pe.wait_ge(a_bd, 2 * b + 2)
                for t in range(TT):
                    mm = nc.tensor.matmul(num_den(0)[:, t, 0:D + H], tiles(q_feat)[:, t, :], kv_bd[:],
                                          start=True, stop=True)
                mm.then_inc(a_num, 1)
                pe.wait_ge(a_o, b + 1)
                for t in range(TT):
                    mm = nc.tensor.transpose(tiles(bank(7))[:, t, :], o_tok[:, t, :], ident[:])
                mm.then_inc(a_oT, 1)
                pe.wait_ge(a_oTc, b + 1)
                for t in range(TT):
                    mm = nc.tensor.matmul(tiles(bank(2))[:, t, :], oT[:, t * 128:(t + 1) * 128], w["w_out"][:],
                                          start=True, stop=True)
                mm.then_inc(a_y, 1)

        def attn_a_vector(v):
            na.vector_stats(v, 1)
            na.vector_hat(v, 1)
            with v.Fori(1, B + 1) as b:
                v.wait_ge(a_q, b + 1)
                nc.vector.tensor_tensor(q_prod[:, 0, :], bank(0), rope_q[:, 0, :], ALU.mult).then_inc(a_prod, 1)
                nc.vector.tensor_tensor(q_prod[:, 1, :], bank(1), rope_q[:, 1, :], ALU.mult).then_inc(a_prod, 1)
                v.wait_ge(a_kv, b + 1)
                nc.vector.tensor_tensor(tiles(k_prod[:, 0, :]), psum[:, 2:2 + TT, 0:D], tiles(rope_k[:, 0, :]),
                                        ALU.mult).then_inc(a_prod, 1)
                nc.vector.tensor_tensor(tiles(k_prod[:, 1, :]), psum[:, 2:2 + TT, 2 * D:3 * D],
                                        tiles(rope_k[:, 1, :]), ALU.mult).then_inc(a_prod, 1)
                for n, prod in enumerate((q_prod, k_prod)):
                    v.wait_ge(a_prod, 4 * b + 2 * n + 2)
                    nc.vector.tensor_tensor(prod[:, 0, :], prod[:, 0, :], prod[:, 1, :], ALU.add).then_inc(a_rope, 1)
                for n, (prod, e) in enumerate(((q_prod, q_exp), (k_prod, k_exp))):
                    v.wait_ge(a_rope, 2 * b + n + 1)
                    nc.vector.tensor_scalar(e, prod[:, 0, :], 0.0, None, ALU.min).then_inc(a_min, 1)
                na.vector_stats(v, b + 1)
                for n, (prod, e, feat) in enumerate(((q_prod, q_exp, q_feat), (k_prod, k_exp, k_feat))):
                    v.wait_ge(a_exp, 2 * b + n + 1)
                    v.wait_ge((a_num, a_sum)[n], b)
                    nc.vector.scalar_tensor_tensor(feat, prod[:, 0, :], 0.0, e, ALU.max, ALU.add).then_inc(a_feat, 1)
                na.vector_hat(v, b + 1)
                v.wait_ge(a_sum, b + 1)
                nc.vector.tensor_tensor(kv_bd[:, 0:D], bank(7, D), const["same_head"][:], ALU.mult).then_inc(a_bd, 1)
                nc.vector.tensor_scalar(kv_bd[:, D:D + H], const["head_mask"][:], psum[:, 7, D:D + 1], None,
                                        ALU.mult).then_inc(a_bd, 1)
                v.wait_ge(a_num, b + 1)
                nc.vector.tensor_scalar(den[:], num_den(0)[:, :, D:D + H], EPS, None, ALU.max).then_inc(a_den, 1)
                v.wait_ge(a_den, b + 1)
                nc.vector.reciprocal(rec[:], den[:]).then_inc(a_rec, 1)
                v.wait_ge(a_rec, b + 1)
                v.wait_ge(a_oT, b)
                nc.vector.tensor_tensor(o_tok[:].rearrange("p t (h d) -> p t h d", d=HD),
                                        num_den(0)[:, :, 0:D].rearrange("p t (h d) -> p t h d", d=HD),
                                        rec[:].unsqueeze(3).broadcast_to([128, TT, H, HD]),
                                        ALU.mult).then_inc(a_o, 1)
                v.wait_ge(a_y, b + 1)
                nc.vector.tensor_tensor(xs(b, 0, TT), bank(2), xs(b, 0, TT), ALU.add).then_inc(a_x, 1)

        def attn_a_scalar(a):
            na.scalar_copy(a, 1, 6)
            with a.Fori(1, B + 1) as b:
                a.wait_ge(a_prod, 4 * b + 4)
                a.wait_ge(a_sum, b)
                nc.scalar.copy(v_ones[:, :, 0:D], psum[:, 2:2 + TT, D:2 * D]).then_inc(a_v, 1)
                for n, e in enumerate((q_exp, k_exp)):
                    a.wait_ge(a_min, 2 * b + n + 1)
                    nc.scalar.activation(e, e, ACT.Exp).then_inc(a_exp, 1)
                na.scalar_copy(a, b + 1, 6)
                a.wait_ge(a_oT, b + 1)
                a.wait_ge(a_y, b)
                nc.scalar.copy(oT[:], bank(7)).then_inc(a_oTc, 1)

        def attn_a_pool(p):
            na.pool_rstd(p, 1)
            with p.Fori(1, B + 1) as b:
                na.pool_rstd(p, b + 1)

        silu_out = ring_a[:, 0:IC * T].rearrange("p (c n) -> p c n", c=IC)
        hidden = ring_a[:, IC * T:3 * IC * T].rearrange("p (e c n) -> p e c n", e=2, c=IC)
        w_parts = stacks[:, 0:4 * E * INNER].rearrange("p (g a e c n) -> p g a e c n", g=2, a=2, e=E, c=IC)
        w_whole = [w[k][:].rearrange("p (e c n) -> p e c n", e=E, c=IC) for k in ("w_gate", "w_up")]
        PRODUCTS = ((0, 0), (0, 1), (1, 0))
        w_down = w["w_down"][:].rearrange("p (e c n) -> p e c n", e=E, c=IC)
        by_expert = lambda ap: ap.rearrange("p (t e) -> p t e", e=ROUTED)
        spread = lambda ap: ap.unsqueeze(2).broadcast_to([128, TT, ROUTED])
        EC = E * IC
        XC = 1 + ROUTED * TT
        LINKS = 17

        class Experts:
            def __init__(self, name, previous):
                self.previous = previous
                self.logits, self.gate_up, self.y = signals("tensor", name, logits=1, gate_up=EC, y=E)
                self.logit_ready, self.chain, self.weight_ready, self.hidden, self.x = signals(
                    "vector", name, logit_ready=1, chain=LINKS, weight_ready=1, hidden=EC, x=XC)
                self.exp_ready, self.silu, self.x_high = signals("scalar", name, exp_ready=1, silu=EC, x_high=1)
                self.x_low, = signals("vector", name, x_low=1)
                self.w_high, self.w_low = signals("scalar", name, passed=0, w_high=1)[0], signals(
                    "vector", name, passed=0, w_low=1)[0]
                self.norm = Norm(name, self.logits, 1)
                self.done = (self.x, (B + 1) * XC, self.norm)

            def tensor_turn(self, pe, n):
                pe.wait_ge(self.x_low, n)
                self.norm.tensor_turn(pe, n, 6)

            def tensor(self, pe):
                after(pe, self.previous)
                self.tensor_turn(pe, 1)
                pe.wait_ge(self.w_low, 2 * E)
                with pe.Fori(1, B + 1) as b:
                    pe.wait_ge(self.norm.xT_ready, b + 1)
                    pe.wait_ge(self.logit_ready, b)
                    for t in range(TT):
                        mm = nc.tensor.matmul(psum[:, 7, t * ROUTED:(t + 1) * ROUTED], xT[:, t * 128:(t + 1) * 128],
                                              w["w_router"][:], start=True, stop=True)
                    mm.then_inc(self.logits, 1)
                    pe.wait_ge(self.x_high, b + 1)
                    pe.wait_ge(self.x_low, b + 1)
                    for e in range(E + 1):
                        if e < E:
                            for c in range(IC):
                                pe.wait_ge(self.hidden, b * EC + max(e * IC + c - 1, 0))
                                for g in range(2):
                                    for n, (wp, xp) in enumerate(PRODUCTS):
                                        mm = nc.tensor.matmul(bank(2 * g + c), w_parts[:, g, wp, e, c, :],
                                                              (x_high, x_low)[xp], start=n == 0, stop=n == 2)
                                mm.then_inc(self.gate_up, 1)
                        if e == E - 1:
                            self.tensor_turn(pe, b + 1)
                        if e > 0:
                            pe.wait_ge(self.hidden, b * EC + e * IC)
                            done = 0 if e < 3 else 1 + (e - 3) * TT
                            pe.wait_ge(self.x, b * XC + done)
                            for t in range(TT):
                                for c in range(IC):
                                    mm = nc.tensor.matmul(tiles(bank(4 + (e - 1) % 2))[:, t, :],
                                                          hidden[:, (e - 1) % 2, c, t * 128:(t + 1) * 128],
                                                          w_down[:, e - 1, c, :], start=c == 0, stop=c == IC - 1)
                            mm.then_inc(self.y, 1)

            def scalar_parts(self, a, n):
                self.norm.scalar_copy(a, n, 6)
                a.wait_ge(self.gate_up, n * EC)
                nc.scalar.copy(x_high, bank(6)).then_inc(self.x_high, 1)

            def scalar(self, a):
                after(a, self.previous)
                for e in range(E):
                    for g in range(2):
                        nc.scalar.copy(w_parts[:, g, 0, e], w_whole[g][:, e]).then_inc(self.w_high, 1)
                self.scalar_parts(a, 1)
                with a.Fori(1, B + 1) as b:
                    a.wait_ge(self.logit_ready, b + 1)
                    nc.scalar.activation(route[:, 0], logit[:], ACT.Exp, scale=-1.0).then_inc(self.exp_ready, 1)
                    for e in range(E):
                        for c in range(IC):
                            a.wait_ge(self.gate_up, b * EC + e * IC + c + 1)
                            a.wait_ge(self.hidden, b * EC + max(e * IC + c - 1, 0))
                            nc.scalar.activation(silu_out[:, c, :], bank(c), ACT.Silu).then_inc(self.silu, 1)
                    self.scalar_parts(a, b + 1)

            def pool(self, p):
                after(p, self.previous)
                self.norm.pool_rstd(p, 1)
                with p.Fori(1, B + 1) as b:
                    self.norm.pool_rstd(p, b + 1)

            def routing(self, v, b, links):
                for n in links:
                    if n == 0:
                        v.wait_ge(self.exp_ready, b + 1)
                    else:
                        v.wait_ge(self.chain, b * LINKS + n)
                    prob, first, second, score = (route[:, k] for k in range(1, 5))
                    left = route[:, 5]
                    rank = by_expert(const["choice_rank"][:])
                    k, (source, chosen) = (0, (prob, first)) if n < 9 else (3, (left, second))
                    tt = nc.vector.tensor_tensor
                    if n == 0:
                        ins = nc.vector.tensor_scalar(score, route[:, 0], 1.0, None, ALU.add)
                    elif n == 1:
                        ins = nc.vector.reciprocal(prob, score)
                    elif n in (2, 8):
                        if n == 8:
                            k, source = 3, left
                        ins = nc.vector.tensor_reduce(best[:, k], source, AX.X, ALU.max)
                    elif n in (3, 9):
                        ins = tt(score, source, spread(best[:, k]), ALU.is_equal)
                    elif n in (4, 10):
                        ins = tt(score, score, rank, ALU.mult)
                    elif n in (5, 11):
                        ins = nc.vector.tensor_reduce(best[:, k + 1], score, AX.X, ALU.max)
                    elif n in (6, 12):
                        ins = tt(chosen, score, spread(best[:, k + 1]), ALU.is_equal)
                    elif n == 7:
                        ins = nc.vector.scalar_tensor_tensor(left, first, -2.0, prob, ALU.mult, ALU.add)
                    elif n == 13:
                        ins = tt(best[:, 2], best[:, 0], best[:, 3], ALU.add)
                    elif n == 14:
                        ins = nc.vector.reciprocal(best[:, 5], best[:, 2])
                    elif n == 15:
                        ins = tt(score, first, second, ALU.add)
                    elif n == 16:
                        ins = tt(score, score, prob, ALU.mult)
                    else:
                        tt(gate_weight[:], score, spread(best[:, 5]), ALU.mult).then_inc(self.weight_ready, 1)
                        continue
                    ins.then_inc(self.chain, 1)

            def vector_parts(self, v, n):
                v.wait_ge(self.x_high, n + 1)
                nc.vector.tensor_tensor(x_low, bank(6), x_high.bitcast(F32), ALU.subtract).then_inc(self.x_low, 1)

            def vector(self, v):
                after(v, self.previous)
                self.norm.vector_stats(v, 1)
                self.norm.vector_hat(v, 1)
                for e in range(E):
                    for g in range(2):
                        v.wait_ge(self.w_high, 2 * e + g + 1)
                        nc.vector.tensor_tensor(w_parts[:, g, 1, e], w_whole[g][:, e], w_parts[:, g, 0, e].bitcast(F32),
                                                ALU.subtract).then_inc(self.w_low, 1)
                self.vector_parts(v, 1)
                with v.Fori(1, B + 1) as b:
                    v.wait_ge(self.logits, b + 1)
                    v.wait_ge(self.exp_ready, b)
                    nc.vector.tensor_tensor(logit[:], by_expert(bank(7, TT * ROUTED)), by_expert(w["router_bias"][:]),
                                            ALU.add).then_inc(self.logit_ready, 1)
                    for e in range(E + 1):
                        if e < E:
                            for c in range(IC):
                                v.wait_ge(self.silu, b * EC + e * IC + c + 1)
                                if c == 0:
                                    v.wait_ge(self.y, b * E + max(e - 1, 0))
                                nc.vector.tensor_tensor(hidden[:, e % 2, c, :], bank(2 + c), silu_out[:, c, :],
                                                        ALU.mult).then_inc(self.hidden, 1)
                                if e < 2:
                                    n = e * IC + c
                                    self.routing(v, b, range((LINKS + 1) * n // 4, (LINKS + 1) * (n + 1) // 4))
                        if e == 4:
                            self.norm.vector_stats(v, b + 1)
                        if e == 6:
                            self.norm.vector_hat(v, b + 1)
                        if e > 0:
                            v.wait_ge(self.y, b * E + e)
                            y = tiles(bank(4 + (e - 1) % 2))
                            if e == 1:
                                nc.vector.tensor_tensor(xs(b, 0, TT), bank(4), xs(b, 0, TT), ALU.add).then_inc(self.x, 1)
                                v.wait_ge(self.weight_ready, b + 1)
                                continue
                            v.wait_ge(self.x, b * XC + 1 + (e - 2) * TT)
                            for t in range(TT):
                                nc.vector.scalar_tensor_tensor(xs(b, t), y[:, t, :], gate_weight[:, t, e - 2:e - 1],
                                                               xs(b, t), ALU.mult, ALU.add).then_inc(self.x, 1)
                        if e == E - 1:
                            self.vector_parts(v, b + 1)

        UNITS = [(k, k) for k in range(TT)] + [(k, q) for k in range(TT) for q in range(k + 1, TT)]
        NA, NB = 2 * TT, len(UNITS) // 2
        KA, KB = NA * GROUPS, NB * GROUPS
        TICKS = "B0 A0 A1 B1 A2 A3 B2 A4 A5 B3 A6 B4 A7".split()
        NT = len(TICKS)
        assert [t for t in TICKS if t[0] == "A"] == [f"A{i}" for i in range(NA)]
        A_STEPS = [(3, 0), (0, 0), (3, 1), (0, 1), (2, 0), (1, 0), (2, 1), (1, 1)]
        BUILD = {0: 0, 7: 1, 10: 2}
        HALVES = {1: (3, 0), 2: (3, 1), 3: (4, 0), 4: (4, 1), 5: (0, 0), 6: (0, 1), 8: (1, 0), 9: (1, 1), 11: (2, 0), 12: (2, 1)}
        LOGS = {2: 0, 5: 1, 8: 2, 11: 3}
        RING = 4
        head_q = stacks[:, 0:H * T].rearrange("p (h n) -> p h n", h=H)
        stack_ky = stacks[:, H * T:(H + 2) * T].rearrange("p (g n) -> p g n", g=2)
        stack_k = stacks[:, (H + 2) * T:].rearrange("p (g n) -> p g n", g=GROUPS)
        high, stack_q = x_high, x_low
        exps = ring_a[:].rearrange("p (r a n) -> p r a n", r=RING, a=2)
        ring = ring_b[:].rearrange("p (r n) -> p r n", r=RING)
        half_sums = sb("half_sums", [OW, 2, T])
        exp_sums, exp_sums_eps, r_tok = (sb(k, [128, TT, 4]) for k in ("exp_sums", "exp_sums_eps", "r_tok"))
        r_rowsT = sb("r_rowsT", [TT * 4, 128])

        def zero_stacks(eng, engine, heads, zeroed):
            engine.memset(head_q[:, heads[0]:heads[1], :].bitcast(F32), 0.0).then_inc(zeroed, 1)

        class LogAttention:
            def __init__(self, previous):
                self.previous = previous
                (self.v_product, self.b_score, self.sum_b, self.num, self.oT, self.y) = signals(
                    "tensor", "b", v_product=1, b_score=KB, sum_b=KB, num=1, oT=1, y=1)
                self.a_score, = signals("tensor", "b", passed=1 / 2, a_score=KA)
                self.r_turned, = signals("tensor", "b", passed=3 / 4, r_turned=4)
                self.stack_product, = signals("tensor", "b", passed=1 / 4, stack_product=3 * GROUPS)
                (self.v_ready, self.ratio, self.den, self.rec, self.o, self.x) = signals(
                    "vector", "b", v_ready=TT, ratio=KB, den=1, rec=1, o=2, x=1)
                self.clip, self.exp_sum = signals("vector", "b", passed=1 / 2, clip=KA, exp_sum=KA)
                self.sum_eps, self.r_ready = signals("vector", "b", passed=3 / 4, sum_eps=4, r_ready=4)
                self.stack, self.head_q = signals("vector", "b", passed=1 / 4, stack=3 * GROUPS, head_q=H)
                self.abs, self.ln, self.half_ready, self.oTc = signals(
                    "scalar", "b", abs=KB, ln=KB, half_ready=2, oTc=1)
                self.exp, = signals("scalar", "b", passed=1 / 2, exp=KA)
                self.r_copied, = signals("scalar", "b", passed=3 / 4, r_copied=4)
                self.high, = signals("scalar", "b", passed=1 / 4, high=3 * GROUPS)
                self.mask_a, = signals("pool", "b", passed=1 / 2, mask_a=KA)
                self.mask_b, = signals("pool", "b", mask_b=2 * GROUPS)
                self.stored, self.spread = sem("b_stored"), sem("b_spread")
                self.zeroed_pool, self.zeroed_vector = sem("b_zeroed_pool"), sem("b_zeroed_vector")
                self.norm = Norm("b", self.stack_product, 3 * GROUPS, 3 * (GROUPS - 1))
                self.go, self.sync_go = sem("b_mask_go"), sem("b_sync_go")
                self.done = (self.x, B + 1, self.norm)

            def spreads(self, b, s):
                return 16 * (4 * (b - 1) + s + 2)

            def build_product(self, pe, b, s, piece):
                if (s, piece) == (0, 0):
                    pe.wait_ge(self.x, b)
                if (s, piece) == (1, 0):
                    pe.wait_ge(self.norm.xT_ready, b + 2)
                pe.wait_ge(self.stack, b * 3 * GROUPS + 3 * s + piece)
                g = (s + 3) % GROUPS
                weight = w[("b_q", "b_ky", "b_k")[piece]]
                nc.tensor.matmul(bank(4), weight[:, g * 128:(g + 1) * 128], xT[:], start=True,
                                 stop=True).then_inc(self.stack_product, 1)

            def score(self, pe, b, s, t, alone=False):
                n = s * NT + t
                kind, i = TICKS[t][0], int(TICKS[t][1])
                before = n - 2
                bs, bt = divmod(before % (GROUPS * NT), NT)
                wrapped = before < 0
                bk, bi = TICKS[bt][0], int(TICKS[bt][1])
                if bk == "A":
                    pe.wait_ge(self.exp, b * KA + bs * NA + bi + 1 - (KA if wrapped else 0))
                else:
                    pe.wait_ge(self.abs, b * KB + bs * NB + bi + 1 - (KB if wrapped else 0))
                if s == 0 and t < 2:
                    pe.wait_ge(self.exp, b * KA)
                if alone:
                    pe.wait_ge(self.exp, b * KA + s * NA + i)
                first = 2 * (n % 2)
                if kind == "A":
                    g, (qb, pair) = (s + 2) % GROUPS, A_STEPS[i]
                    if i == 0:
                        pe.wait_ge(self.stack, b * 3 * GROUPS + 3 * s)
                        pe.wait_ge(self.head_q, b * H + 4 * s)
                    for h in range(2):
                        mm = nc.tensor.matmul(bank(first + h, (qb + 1) * 128),
                                              head_q[:, 4 * g + 2 * pair + h, qb * 128:(qb + 1) * 128],
                                              stack_ky[:, (s + 1) % 2, 0:(qb + 1) * 128], start=True, stop=True)
                    mm.then_inc(self.a_score, 1)
                else:
                    for m, (kb, qb) in enumerate(UNITS[2 * i:2 * i + 2]):
                        mm = nc.tensor.matmul(bank(first + m), stack_k[:, s, kb * 128:(kb + 1) * 128],
                                              head_q[:, 4 * s:4 * s + 4, qb * 128:(qb + 1) * 128],
                                              start=True, stop=True)
                    mm.then_inc(self.b_score, 1)

            def weighted_values(self, pe, b, s, i, m):
                if (s, i, m) == (0, 0, 0):
                    pe.wait_ge(self.v_ready, (b + 1) * TT)
                    pe.wait_ge(self.o, 2 * b)
                if m == 0 and i < 2:
                    pe.wait_ge(self.mask_b, b * 2 * GROUPS + 2 * s + i + 1)
                elif m == 0:
                    pe.wait_ge(self.ln, b * KB + s * NB + i + 1)
                first, last = s % 2 == 0 and i == 0, s % 2 == 1 and i == NB - 1
                kb, qb = UNITS[2 * i + m]
                for h in range(4):
                    mm = nc.tensor.matmul(psum[0:OW, 5 + s // 2, qb * 128:(qb + 1) * 128],
                                          values[:, kb, 4 * s + h, :],
                                          ring[:, (s * NB + i) % RING, m * T + h * 128:m * T + (h + 1) * 128],
                                          start=first and m == 0 and h == 0,
                                          stop=last and m == 1 and h == 3, skip_group_check=True)
                if m == 1:
                    mm.then_inc(self.sum_b, 1)

            def turn_r(self, pe, b, s):
                pe.wait_ge(self.r_ready, b * 4 + s + 1)
                pe.wait_ge(self.r_copied, b * 4 + s)
                if s == 0:
                    pe.wait_ge(self.v_ready, (b + 1) * TT)
                if s == 1:
                    pe.wait_ge(self.norm.xT_ready, b + 2)
                nc.tensor.transpose(psum[0:TT * 4, 7, 0:128], r_tok[:].rearrange("p t h -> p (t h)"),
                                    ident[:]).then_inc(self.r_turned, 1)

            def tensor_slot(self, pe, b, s, stage_b=True, stage_a=True, chain=True):
                for t, tick in enumerate(TICKS):
                    if (stage_a if tick[0] == "A" else stage_b):
                        self.score(pe, b, s, t, alone=not stage_b)
                    if t in BUILD:
                        self.build_product(pe, b, s, BUILD[t])
                    if t == 3 and chain:
                        self.turn_r(pe, b, s)
                    if not stage_b:
                        continue
                    if t == 8 and s == 0:
                        pe.wait_ge(self.r_copied, b * 4 + 1)
                        self.norm.tensor_turn(pe, b + 1, 7)
                    if t in HALVES and (t > 4 or s > 0):
                        i, m = HALVES[t]
                        self.weighted_values(pe, b, s - (t <= 4), i, m)

            def tensor(self, pe):
                after(pe, self.previous)
                self.norm.tensor_turn(pe, 1, 7)
                self.tensor_slot(pe, 0, 1, stage_b=False, stage_a=False, chain=False)
                self.tensor_slot(pe, 0, 2, stage_b=False, chain=False)
                self.tensor_slot(pe, 0, 3, stage_b=False)
                with pe.Fori(1, B + 1) as b:
                    pe.wait_ge(self.r_copied, b * 4)
                    pe.wait_ge(self.oTc, b)
                    for t in range(TT):
                        mm = nc.tensor.matmul(tiles(bank(7))[:, t, :], xT[:, t * 128:(t + 1) * 128],
                                              w["b_v"][:], start=True, stop=True)
                    mm.then_inc(self.v_product, 1)
                    for s in range(GROUPS):
                        self.tensor_slot(pe, b, s)
                    for i in (3, 4):
                        for m in range(2):
                            self.weighted_values(pe, b, GROUPS - 1, i, m)
                    pe.wait_ge(self.half_ready, 2 * b + 2)
                    for t in range(TT):
                        for half in range(2):
                            mm = nc.tensor.transpose(num_den(5)[:, t, half * OW:(half + 1) * OW],
                                                     half_sums[:, half, t * 128:(t + 1) * 128], ident[0:OW, 0:OW])
                    mm.then_inc(self.num, 1)
                    pe.wait_ge(self.o, 2 * b + 2)
                    pe.wait_ge(self.r_copied, b * 4 + 4)
                    for t in range(TT):
                        mm = nc.tensor.transpose(tiles(bank(7))[:, t, :], o_tok[:, t, :], ident[:])
                    mm.then_inc(self.oT, 1)
                    pe.wait_ge(self.oTc, b + 1)
                    pe.wait_ge(self.stack, (b + 1) * 3 * GROUPS)
                    for t in range(TT):
                        mm = nc.tensor.matmul(tiles(bank(4))[:, t, :], oT[:, t * 128:(t + 1) * 128], w["b_proj"][:],
                                              start=True, stop=True)
                    mm.then_inc(self.y, 1)

            def logarithm(self, a, b, s, i):
                a.wait_ge(self.ratio, b * KB + s * NB + i + 1)
                r = ring[:, (s * NB + i) % RING, :]
                nc.scalar.activation(r, r, ACT.Ln, bias=1.0).then_inc(self.ln, 1)

            def scalar_slot(self, a, b, s, stage_b=True, stage_a=True, chain=True):
                for t, tick in enumerate(TICKS):
                    kind, i = tick[0], int(tick[1])
                    first = 2 * ((s * NT + t) % 2)
                    if kind == "A" and stage_a:
                        a.wait_ge(self.a_score, b * KA + s * NA + i + 1)
                        a.wait_ge(self.exp_sum, b * KA + s * NA + i + 1 - RING)
                        width = (A_STEPS[i][0] + 1) * 128
                        nc.scalar.activation(exps[:, i % RING, :, 0:width], psum[:, first:first + 2, 0:width],
                                             ACT.Exp, scale=SCALE).then_inc(self.exp, 1)
                    if kind == "B" and stage_b:
                        step = s * NB + i
                        a.wait_ge(self.b_score, b * KB + step + 1)
                        a.wait_ge(self.sum_b, b * KB + step + 1 - RING)
                        nc.scalar.activation(ring[:, step % RING, :].rearrange("p (a n) -> p a n", a=2),
                                             psum[:, first:first + 2, :], ACT.Abs, scale=SCALE).then_inc(self.abs, 1)
                    if t in BUILD:
                        a.wait_ge(self.stack_product, b * 3 * GROUPS + 3 * s + BUILD[t] + 1)
                        nc.scalar.copy(high, bank(4)).then_inc(self.high, 1)
                    if t == 4 and chain:
                        a.wait_ge(self.r_turned, b * 4 + s + 1)
                        if stage_b:
                            a.wait_ge(self.stored, self.spreads(b, s) - 16)
                        nc.scalar.copy(r_rowsT[:], psum[0:TT * 4, 7, 0:128]).then_inc(self.r_copied, 1)
                    if not stage_b:
                        continue
                    if t == 0 and s > 0:
                        self.logarithm(a, b, s - 1, NB - 1)
                    if t in LOGS:
                        self.logarithm(a, b, s, LOGS[t])
                    if t == 12 and s == 0:
                        self.norm.scalar_copy(a, b + 1, 7)
                    if t == 7 and s == 2:
                        self.copy_half(a, b, 0)

            def copy_half(self, a, b, half):
                a.wait_ge(self.sum_b, b * KB + (half + 1) * KB // 2)
                a.wait_ge(self.num, b)
                nc.scalar.copy(half_sums[:, half, :], psum[0:OW, 5 + half, :]).then_inc(self.half_ready, 1)

            def scalar(self, a):
                after(a, self.previous)
                nc.scalar.preload_act_table_set("natural_log_exp_and_others")
                self.norm.scalar_copy(a, 1, 7)
                self.scalar_slot(a, 0, 1, stage_b=False, stage_a=False, chain=False)
                self.scalar_slot(a, 0, 2, stage_b=False, chain=False)
                self.scalar_slot(a, 0, 3, stage_b=False)
                with a.Fori(1, B + 1) as b:
                    for s in range(GROUPS):
                        self.scalar_slot(a, b, s)
                    self.logarithm(a, b, GROUPS - 1, NB - 1)
                    self.copy_half(a, b, 1)
                    a.wait_ge(self.oT, b + 1)
                    a.wait_ge(self.y, b)
                    nc.scalar.copy(oT[:], bank(7)).then_inc(self.oTc, 1)

            def build_stack(self, v, b, s, piece):
                g = (s + 3) % GROUPS
                v.wait_ge(self.high, b * 3 * GROUPS + 3 * s + piece + 1)
                if piece == 1:
                    v.wait_ge(self.a_score, b * KA + s * NA)
                if piece == 2:
                    v.wait_ge(self.b_score, b * KB + s * NB)
                out = (stack_q, stack_ky[:, s % 2, :], stack_k[:, g, :])[piece]
                nc.vector.scalar_tensor_tensor(out, high.bitcast(F32), const["minus_low"][:, min(piece, 1):min(piece, 1) + 1],
                                               bank(4), ALU.mult, ALU.add).then_inc(self.stack, 1)
                if piece == 0:
                    v.wait_ge(self.stack, b * 3 * GROUPS + 3 * s + 1)
                    v.wait_ge(self.b_score, b * KB + s * NB)
                    for j in range(4):
                        rows = slice(32 * j, 32 * (j + 1))
                        nc.vector.tensor_copy(head_q[rows, 4 * g + j, :], stack_q[rows, :].bitcast(F32)
                                              ).then_inc(self.head_q, 1)

            def sum_exps(self, v, b, s, i):
                qb, pair = A_STEPS[i]
                v.wait_ge(self.mask_a, b * KA + s * NA + i + 1)
                nc.vector.tensor_reduce(exp_sums[:, qb, 2 * pair:2 * pair + 2],
                                        exps[:, i % RING, :, 0:(qb + 1) * 128], AX.X, ALU.add).then_inc(self.exp_sum, 1)

            def vector_slot(self, v, b, s, stage_b=True, stage_a=True, chain=True):
                if chain:
                    self.sum_exps(v, b, s - 1, NA - 1)
                    v.wait_ge(self.exp_sum, b * KA + s * NA)
                    nc.vector.tensor_scalar(exp_sums_eps[:], exp_sums[:], EPS, None, ALU.add).then_inc(self.sum_eps, 1)
                    v.wait_ge(self.sum_eps, b * 4 + s + 1)
                    v.wait_ge(self.r_turned, b * 4 + s)
                    nc.vector.reciprocal(r_tok[:], exp_sums_eps[:]).then_inc(self.r_ready, 1)
                for t, tick in enumerate(TICKS):
                    kind, i = tick[0], int(tick[1])
                    if kind == "A" and stage_a:
                        e = exps[:, i % RING, :, 0:(A_STEPS[i][0] + 1) * 128]
                        v.wait_ge(self.exp, b * KA + s * NA + i + 1)
                        nc.vector.tensor_scalar(e, e, CLIP_HI, CLIP_LO, ALU.min, ALU.max).then_inc(self.clip, 1)
                        if i > 0:
                            self.sum_exps(v, b, s, i - 1)
                    if kind == "B" and stage_b:
                        step = s * NB + i
                        v.wait_ge(self.abs, b * KB + step + 1)
                        if i == 0:
                            v.wait_ge(self.spread, self.spreads(b, s) - 16)
                        for m, (kb, qb) in enumerate(UNITS[2 * i:2 * i + 2]):
                            part = ring[:, step % RING, m * T:(m + 1) * T]
                            ins = nc.vector.scalar_tensor_tensor(part, part, EPS, r_rows[:, s % 2, qb * T:(qb + 1) * T],
                                                                 ALU.add, ALU.mult)
                        ins.then_inc(self.ratio, 1)
                    if t - 1 in BUILD:
                        self.build_stack(v, b, s, BUILD[t - 1])
                    if not stage_b:
                        continue
                    if t == 2 and s == 0:
                        self.norm.vector_stats(v, b + 1)
                    if t == 6 and s == 0:
                        self.norm.vector_hat(v, b + 1)

            def vector(self, v):
                after(v, self.previous)
                self.norm.vector_stats(v, 1)
                self.norm.vector_hat(v, 1)
                zero_stacks(v, nc.vector, (H // 2, H), self.zeroed_vector)
                v.wait_ge(self.zeroed_vector, 1)
                v.wait_ge(self.zeroed_pool, 1)
                self.vector_slot(v, 0, 1, stage_b=False, stage_a=False, chain=False)
                self.vector_slot(v, 0, 2, stage_b=False, chain=False)
                self.vector_slot(v, 0, 3, stage_b=False)
                with v.Fori(1, B + 1) as b:
                    v.wait_ge(self.v_product, b + 1)
                    v.wait_ge(self.sum_b, b * KB)
                    for t in range(TT):
                        for half in range(2):
                            dst = values[:, t, half * HALF:(half + 1) * HALF, :].rearrange("p h n -> p (h n)")
                            dst = diagonal(dst)
                            ins = nc.vector.tensor_copy(dst, psum[:, 7, t * D + half * HALF * HD:
                                                                  t * D + (half + 1) * HALF * HD]
                                                        .rearrange("p (h d) -> p h d", d=HD))
                        ins.then_inc(self.v_ready, 1)
                    for s in range(GROUPS):
                        self.vector_slot(v, b, s)
                    v.wait_ge(self.num, b + 1)
                    halves = num_den(5)[:, :, 0:OT].rearrange("p t (a n) -> p t a n", a=2)
                    nc.vector.tensor_scalar(den[:].rearrange("p t (a h) -> p t a h", a=2),
                                            halves[:, :, :, HALF * HD:OW], EPS, None, ALU.add).then_inc(self.den, 1)
                    v.wait_ge(self.den, b + 1)
                    nc.vector.reciprocal(rec[:], den[:]).then_inc(self.rec, 1)
                    v.wait_ge(self.rec, b + 1)
                    v.wait_ge(self.oT, b)
                    for half in range(2):
                        lo, hi = half * HALF, (half + 1) * HALF
                        nc.vector.tensor_tensor(
                            o_tok[:, :, lo * HD:hi * HD].rearrange("p t (h d) -> p t h d", d=HD),
                            halves[:, :, half, 0:HALF * HD].rearrange("p t (h d) -> p t h d", d=HD),
                            rec[:, :, lo:hi].unsqueeze(3).broadcast_to([128, TT, HALF, HD]),
                            ALU.mult).then_inc(self.o, 1)
                    v.wait_ge(self.mask_a, (b + 1) * KA)
                    v.wait_ge(self.y, b + 1)
                    nc.vector.tensor_tensor(xs(b, 0, TT), bank(4), xs(b, 0, TT), ALU.add).then_inc(self.x, 1)

            def pool_slot(self, p, b, s, stage_b=True):
                for tick in "A0 A1 B0 A2 A3 B1 A4 A5 A6 A7".split():
                    kind, i = tick[0], int(tick[1])
                    if kind == "A":
                        p.wait_ge(self.clip, b * KA + s * NA + i + 1)
                        p.sem_inc(self.go, 1)
                        qb = A_STEPS[i][0]
                        e = exps[:, i % RING, :, qb * 128:(qb + 1) * 128]
                        nc.gpsimd.affine_select(out=e, in_=e, pattern=[[0, 2], [-1, 128]], compare_op=ALU.is_ge,
                                                fill=0.0, base=0, channel_multiplier=1).then_inc(self.mask_a, 1)
                    elif stage_b:
                        p.wait_ge(self.ln, b * KB + s * NB + i + 1)
                        p.sem_inc(self.go, 1)
                        r = ring[:, (s * NB + i) % RING, :].rearrange("p (u n) -> p u n", n=128)
                        nc.gpsimd.affine_select(out=r, in_=r, pattern=[[0, 8], [1, 128]], compare_op=ALU.is_ge,
                                                fill=0.0, base=0, channel_multiplier=-1).then_inc(self.mask_b, 1)
                    if tick == "A3" and stage_b and s == 0:
                        self.norm.pool_rstd(p, b + 1)

            def pool(self, p):
                after(p, self.previous)
                self.norm.pool_rstd(p, 1)
                zero_stacks(p, nc.gpsimd, (0, H // 2), self.zeroed_pool)
                self.pool_slot(p, 0, 2, stage_b=False)
                self.pool_slot(p, 0, 3, stage_b=False)
                with p.Fori(1, B + 1) as b:
                    for s in range(GROUPS):
                        self.pool_slot(p, b, s)

            def spread_r(self, sp, b, s, first=False):
                if not first:
                    sp.wait_ge(self.spread, self.spreads(b, s) - 16)
                    sp.sem_inc(self.sync_go, 1)
                sp.wait_ge(self.r_copied, b * 4 + s + 1)
                sp.sem_inc(self.sync_go, 1)
                sp.dma_start(dram_r, r_rowsT[:]).then_inc(self.stored, 16)
                sp.wait_ge(self.stored, self.spreads(b, s))
                sp.sem_inc(self.sync_go, 1)
                sp.wait_ge(self.ratio, b * KB + s * NB)
                sp.sem_inc(self.sync_go, 1)
                sp.dma_start(r_rows[:, (s + 1) % 2, :],
                             dram_r.rearrange("h n -> (h n)").unsqueeze(0).broadcast_to([128, GROUPS * T])
                             ).then_inc(self.spread, 16)

            def sync(self, sp):
                after(sp, self.previous)
                self.spread_r(sp, 0, 3, first=True)
                with sp.Fori(1, B + 1) as b:
                    for s in range(GROUPS):
                        self.spread_r(sp, b, s)
                sp.wait_ge(self.spread, 16 * (4 * B + 1))

        def diagonal(ap):
            return bass.AP(ap.tensor, ap.offset, [ap.ap[0], [OW + HD, HALF], [1, HD]])

        ffn_1 = Experts("f1", (a_x, B + 1, na))
        log_attn = LogAttention(ffn_1.done)
        ffn_2 = Experts("f2", log_attn.done)
        stored, store_go = sem("stored"), sem("store_go")

        block = ctx.enter_context(nc.Block())

        @block.sync
        def _(s):
            def load(name, signal):
                dst = {"rope_q": ring_b[:, 0:2 * T], "rope_k": ring_b[:, 2 * T:2 * T + 2 * TT * D]}.get(name)
                if dst is None:
                    dst = (const[name] if name in const else w[name])[:]
                s.dma_start(dst, ins[name]).then_inc(signal, 16)

            for n in range(B):
                if n == 1:
                    for name in first_loads:
                        load(name, loaded_first)
                s.dma_start(tiles(x_res[:, n * TT * D:(n + 1) * TT * D]),
                            x_in[n * T:(n + 1) * T, :].rearrange("(t p) d -> p t d", p=128)
                            ).then_inc(loaded_x0 if n == 0 else loaded_x, 16)
            for name in rest_loads:
                load(name, loaded)
            log_attn.sync(s)
            after(s, log_attn.done)
            with s.Fori(1, B + 1) as b:
                target = out[bass.ds((b - 1) * T, T), :].rearrange("(t p) d -> p t d", p=128)
                source = tiles(xs(b, 0, TT))
                s.wait_ge(ffn_2.x, (b + 1) * XC)
                s.sem_inc(store_go, 1)
                s.dma_start(target, source).then_inc(stored, 16)
            s.wait_ge(stored, 16 * B)

        @block.gpsimd
        def _(p):
            start(p, "pool")
            nc.gpsimd.memset(neg_half[:], -0.5).then_inc(setup, 1)
            nc.gpsimd.memset(x_res[:, B * TT * D:], 0.0).then_inc(setup, 1)
            nc.gpsimd.memset(v_ones[:, :, D:D + 1], 1.0).then_inc(setup, 1)
            nc.gpsimd.memset(values[:], 0.0).then_inc(setup, 1)
            p.wait_ge(setup, 4)
            for half in range(2):
                for t in range(TT):
                    block_of = values[:, t, half * HALF:(half + 1) * HALF, :].rearrange("p h n -> p (h n)")
                    nc.gpsimd.memset(bass.AP(block_of.tensor, block_of.offset + HALF * HD,
                                             [block_of.ap[0], [OW + 1, HALF], [1, 1]]), 1.0).then_inc(setup, 1)
            attn_a_pool(p)
            ffn_1.pool(p)
            log_attn.pool(p)
            ffn_2.pool(p)

        @block.vector
        def _(v):
            start(v, "vector")
            v.wait_ge(setup, SETUP)
            v.wait_ge(loaded_x0, 16)
            v.wait_ge(loaded_first, 16 * len(first_loads))
            v.wait_ge(loaded_x, 16 * (B - 1))
            attn_a_vector(v)
            v.wait_ge(loaded, 16 * len(rest_loads))
            ffn_1.vector(v)
            log_attn.vector(v)
            ffn_2.vector(v)

        @block.scalar
        def _(a):
            start(a, "scalar")
            a.wait_ge(setup, SETUP)
            attn_a_scalar(a)
            a.wait_ge(loaded, 16 * len(rest_loads))
            ffn_1.scalar(a)
            log_attn.scalar(a)
            ffn_2.scalar(a)

        @block.tensor
        def _(pe):
            start(pe, "tensor")
            pe.wait_ge(setup, SETUP)
            pe.wait_ge(loaded_first, 16 * len(first_loads))
            attn_a_tensor(pe)
            pe.wait_ge(loaded, 16 * len(rest_loads))
            ffn_1.tensor(pe)
            log_attn.tensor(pe)
            ffn_2.tensor(pe)


def lay_out(inputs):
    w_qkv = inputs["L0_attn_a_W_qkv"]
    turned = np.arange(D).reshape(H, 2, HD // 2)[:, ::-1].reshape(-1)

    stacked = np.tile(np.arange(D).reshape(H, 1, HD), (1, PARTS, 1)).reshape(-1)

    def with_shared(shared, routed):
        return np.concatenate([shared[None], routed], 0)

    gate = with_shared(inputs["L0_ffn_sg_w"], inputs["L0_ffn_wg"])
    up = with_shared(inputs["L0_ffn_su_w"], inputs["L0_ffn_wu"])
    down = with_shared(inputs["L0_ffn_sd_w"], inputs["L0_ffn_wd"])
    laid = {
        "w_qkv": w_qkv,
        "w_qk_rot": np.concatenate([w_qkv[:, :D][:, turned], w_qkv[:, D:2 * D][:, turned]], 1),
        "w_out": inputs["L0_attn_a_W_out"],
        "b_q": inputs["L0_attn_b_w_qkv"][:D].T[:, stacked],
        "b_ky": inputs["L0_attn_b_w_ky"].T[:, stacked],
        "b_k": inputs["L0_attn_b_w_qkv"][D:2 * D].T[:, stacked],
        "b_v": inputs["L0_attn_b_w_qkv"][2 * D:].T,
        "b_proj": inputs["L0_attn_b_w_proj"].T,
        "w_gate": gate.transpose(2, 0, 1).reshape(D, -1),
        "w_up": up.transpose(2, 0, 1).reshape(D, -1),
        "w_down": down.reshape(E, D, IC, 128).transpose(3, 0, 2, 1).reshape(128, -1),
        "w_router": inputs["L0_ffn_router_w"].T,
        "router_bias": np.tile(inputs["L0_ffn_routing_bias"], (128, TT)),
    }
    return {k: np.ascontiguousarray(v) for k, v in laid.items()}


def kernel(**inputs):
    from concourse import bacc
    from concourse.bass_utils import run_bass_kernel_spmd

    inputs = {k: np.asarray(v) for k, v in inputs.items()}
    arrays = {"x": np.ascontiguousarray(inputs["L0_attn_a_x"].reshape(B * T, D)), **shape_constants(), **lay_out(inputs)}
    nc = bacc.Bacc("TRN2", target_bir_lowering=False, num_devices=1)
    dram = {k: nc.dram_tensor(f"in_{k}", a.shape, mybir.dt.from_np(a.dtype), kind="ExternalInput").ap()
            for k, a in arrays.items()}
    out = nc.dram_tensor("out", (B * T, D), F32, kind="ExternalOutput").ap()
    build(nc, dram["x"], dram, out)
    result = run_bass_kernel_spmd(nc, [{f"in_{k}": a for k, a in arrays.items()}], core_ids=[0])
    return result.results[0]["out"].reshape(B, T, D)
```

```python
from contextlib import ExitStack

import numpy as np

import concourse.bass as bass
from concourse import mybir

F32 = mybir.dt.float32
F32R = mybir.dt.float32r
ALU = mybir.AluOpType
ACT = mybir.ActivationFunctionType
AX = mybir.AxisListType

B, T, D = 8, 512, 128
H, HD = 16, 8
TT = T // 128
E, INNER = 9, 256
IC = INNER // 128
ROUTED = E - 1
SCALE = HD ** -0.5
LN_EPS = 1e-5
EPS = 1e-6
CLIP_LO, CLIP_HI = float(np.exp(np.float32(-15.0))), float(np.exp(np.float32(15.0)))
ROPE_BASE = 500000.0
GROUPS = H // 4
PARTS = 4
HALF = H // 2
OW = HALF * HD + HALF
OT = 2 * OW


def shape_constants():
    inv_freq = (1.0 / ROPE_BASE ** (np.arange(0, HD, 2, dtype=np.float32) / HD)).astype(np.float32)
    freqs = np.arange(T, dtype=np.float32)[:, None] * inv_freq[None, :]
    emb = np.concatenate([freqs, freqs], axis=-1).astype(np.float32)
    sign = np.where(np.arange(HD) < HD // 2, -1.0, 1.0).astype(np.float32)
    cos = np.tile(np.cos(emb), (1, H)).astype(np.float32)
    sin = np.tile(np.sin(emb) * sign, (1, H)).astype(np.float32)
    tables = {
        "rope_q": np.stack([cos.T * np.float32(SCALE), sin.T * np.float32(SCALE)], 1),
        "rope_k": np.stack([cos.reshape(TT, 128, D), sin.reshape(TT, 128, D)], 0)
        .transpose(2, 0, 1, 3),
        "identity": np.eye(128, dtype=np.float32),
    }
    head_of = np.arange(D) // HD
    tables["same_head"] = (head_of[:, None] == head_of[None, :]).astype(np.float32)
    tables["head_mask"] = (head_of[:, None] == np.arange(H)[None, :]).astype(np.float32)
    rows = np.array([[0, 0], [1, 0], [0, 1], [1, 1]], dtype=np.float32)
    low = np.tile(np.repeat(rows, HD, axis=0), (4, 1))
    tables["minus_low"] = np.concatenate([-np.diag(low[:, n]) for n in range(2)], axis=1)
    tables["upper"] = np.concatenate([np.ones((128, T - 128)), np.tril(np.ones((128, 128)))], 1) * CLIP_HI
    tables["choice_rank"] = np.tile(np.arange(ROUTED, 0, -1, dtype=np.float32), (128, TT))
    return {k: np.ascontiguousarray(v, dtype=np.float32).reshape(v.shape[0], -1) for k, v in tables.items()}


CONSTANTS = {"rope_q": 2 * T, "rope_k": 2 * TT * D, "identity": 128, "same_head": D, "head_mask": H,
             "minus_low": 2 * 128,
             "choice_rank": TT * ROUTED, "upper": T}
WEIGHTS = {"w_qk_rot": 2 * D, "w_qkv": 3 * D, "w_out": D, "b_q": GROUPS * 128, "b_ky": GROUPS * 128,
           "b_k": GROUPS * 128, "b_v": D, "b_proj": D,
           "w_gate": E * INNER, "w_up": E * INNER, "w_down": E * IC * D, "w_router": ROUTED,
           "router_bias": TT * ROUTED}


def build(nc, x_in, ins, out):
    ctx = ExitStack()
    with ctx:
        def sb(name, shape, dtype=F32):
            return ctx.enter_context(nc.sbuf_tensor(name, shape, dtype))

        def sem(name):
            return ctx.enter_context(nc.semaphore(name))

        psum = ctx.enter_context(nc.psum_tensor("psum", [128, 8, 512], F32))

        def bank(n, width=512):
            return psum[:, n, 0:width]

        x_res = sb("x_res", [128, (B + 2) * TT * D])
        const = {k: sb(k, [128, w]) for k, w in CONSTANTS.items() if not k.startswith("rope")}
        w = {k: sb(k, [128, n]) for k, n in WEIGHTS.items()}
        ident = const["identity"]
        stats = sb("stats", [128, TT, 6])
        mean_var = sb("mean_var", [128, TT, 2])
        var_eps = sb("var_eps", [128, TT])
        neg_half = sb("neg_half", [128, TT])
        rstd = sb("rstd", [128, TT])
        x_hat = sb("x_hat", [128, TT, D])
        xT = sb("xT", [128, T])

        def xs(n, t=0, tiles=1):
            return x_res[:, bass.ds((n - 1) * (TT * D) + t * D, tiles * D)]

        starts = {engine: [] for engine in ("tensor", "vector", "scalar", "pool")}

        def signals(engine, prefix, passed=1.0, **steps):
            made = [(sem(f"{prefix}_{name}"), k) for name, k in steps.items()]
            starts[engine] += [(s, int(k * passed)) for s, k in made if int(k * passed)]
            return [s for s, _ in made]

        def start(eng, engine):
            for s, k in starts[engine]:
                eng.sem_inc(s, k)

        stacks = sb("stacks", [128, (H + 2 + GROUPS) * T], F32R)
        x_high, x_low = (sb(k, [128, T], F32R)[:] for k in ("x_high", "x_low"))
        ring_a = sb("ring_a", [128, 8 * T])
        ring_b = sb("ring_b", [128, 8 * T])
        r_rows = sb("r_rows", [128, 2, GROUPS * T])
        values = sb("values", [128, TT, H, OW])
        kv_bd = sb("kv_bd", [128, D + H])
        oT = sb("oT", [128, T])
        o_tok = sb("o_tok", [128, TT, D])
        den = sb("den", [128, TT, H])
        rec = sb("rec", [128, TT, H])
        logit = sb("logit", [128, TT, ROUTED])
        route = sb("route", [128, 6, TT, ROUTED])
        best = sb("best", [128, 6, TT])
        gate_weight = sb("gate_weight", [128, TT, ROUTED])
        dram_r = nc.dram_tensor("r_scratch", (H, 128), F32, kind="Internal").ap()

        loaded_x0, loaded_x, loaded_first, loaded = (sem(k) for k in ("loaded_x0", "loaded_x", "loaded_first", "loaded"))
        setup = sem("setup")
        SETUP = 4 + 2 * TT
        first_loads = ["identity", "w_qkv", "w_qk_rot", "rope_q", "rope_k", "same_head", "w_out", "head_mask"]
        rest_loads = [k for k in [*const, *w] if k not in first_loads]

        class Norm:

            def __init__(self, name, used, used_count, used_before=0):
                self.used, self.used_count, self.used_before = used, used_count, used_before
                self.stats_done, self.mean_done, self.var_ready, self.hat_ready = signals(
                    "vector", name, stats_done=TT, mean_done=TT, var_ready=1, hat_ready=TT)
                self.rstd_ready, = signals("pool", name, rstd_ready=1)
                self.turned, = signals("tensor", name, turned=1)
                self.xT_ready, = signals("scalar", name, xT_ready=1)
                self.go = sem(f"{name}_go")

            def vector_stats(self, v, n):
                for t in range(TT):
                    nc.vector.bn_stats(stats[:, t, :], xs(n, t)).then_inc(self.stats_done, 1)
                v.wait_ge(self.stats_done, n * TT + TT)
                v.wait_ge(self.hat_ready, n * TT)
                v.sem_inc(self.go, 1)
                for t in range(TT):
                    nc.vector.bn_aggr(mean_var[:, t, :], stats[:, t, :]).then_inc(self.mean_done, 1)
                v.wait_ge(self.mean_done, n * TT + TT)
                nc.vector.tensor_scalar(var_eps[:], mean_var[:, :, 1], LN_EPS, None, ALU.add).then_inc(self.var_ready, 1)

            def pool_rstd(self, p, n):
                p.wait_ge(self.var_ready, n + 1)
                nc.gpsimd.tensor_tensor(rstd[:], var_eps[:], neg_half[:], ALU.pow).then_inc(self.rstd_ready, 1)

            def vector_hat(self, v, n):
                v.wait_ge(self.rstd_ready, n + 1)
                v.wait_ge(self.turned, n)
                for t in range(TT):
                    nc.vector.tensor_scalar(x_hat[:, t, :], xs(n, t), mean_var[:, t, 0:1], rstd[:, t:t + 1],
                                            ALU.subtract, ALU.mult).then_inc(self.hat_ready, 1)

            def tensor_turn(self, pe, n, to):
                pe.wait_ge(self.hat_ready, n * TT + TT)
                pe.wait_ge(self.xT_ready, n)
                for t in range(TT):
                    mm = nc.tensor.transpose(bank(to)[:, t * 128:(t + 1) * 128], x_hat[:, t, :], ident[:])
                mm.then_inc(self.turned, 1)

            def scalar_copy(self, a, n, frm):
                a.wait_ge(self.turned, n + 1)
                a.wait_ge(self.used, n * self.used_count - self.used_before)
                nc.scalar.copy(xT[:], bank(frm)).then_inc(self.xT_ready, 1)

        def num_den(first_bank):
            return psum[:, first_bank:first_bank + 2, :].rearrange("p b (t n) -> p (b t) n", t=2)

        def after(eng, previous):
            if previous:
                x_done, count, norm, turns = previous
                eng.wait_ge(x_done, count)
                eng.wait_ge(norm.xT_ready, turns)

        a_q, a_kv, a_sum, a_num, a_oT, a_y = signals("tensor", "a", q=1, kv=1, sum=1, num=1, oT=1, y=1)
        a_prod, a_rope, a_min, a_feat, a_bd, a_den, a_rec, a_o, a_x = signals(
            "vector", "a", prod=4, rope=2, min=2, feat=2, bd=2, den=1, rec=1, o=1, x=1)
        a_exp, a_v, a_oTc = signals("scalar", "a", exp=2, v=1, oTc=1)
        na = Norm("a", a_kv, 1)
        q_prod = ring_a[:, 0:2 * T].rearrange("p (a n) -> p a n", a=2)
        k_prod = ring_a[:, 2 * T:4 * T].rearrange("p (a n) -> p a n", a=2)
        q_exp, k_exp = ring_a[:, 4 * T:5 * T], ring_a[:, 5 * T:6 * T]
        q_feat, k_feat = ring_a[:, 6 * T:7 * T], ring_a[:, 7 * T:8 * T]
        v_ones = r_rows[:, 0, 0:TT * (D + 1)].rearrange("p (t n) -> p t n", t=TT)
        rope_q = ring_b[:, 0:2 * T].rearrange("p (a n) -> p a n", a=2)
        rope_k = ring_b[:, 2 * T:2 * T + 2 * TT * D].rearrange("p (a n) -> p a n", a=2)
        tiles = lambda ap: ap.rearrange("p (t n) -> p t n", t=TT)

        def a_sums(pe, b):
            pe.wait_ge(a_feat, 2 * b)
            pe.wait_ge(a_v, b)
            for t in range(TT):
                mm = nc.tensor.matmul(bank(5, D + 1), tiles(k_feat)[:, t, :], v_ones[:, t, :],
                                      start=t == 0, stop=t == TT - 1)
            mm.then_inc(a_sum, 1)

        def a_numerators(pe, b):
            pe.wait_ge(a_bd, 2 * b)
            for t in range(TT):
                mm = nc.tensor.matmul(num_den(5)[:, t, 0:D + H], tiles(q_feat)[:, t, :], kv_bd[:],
                                      start=True, stop=True)
            mm.then_inc(a_num, 1)

        def a_output(pe, b):
            pe.wait_ge(a_o, b)
            pe.wait_ge(na.xT_ready, b + 1)
            for t in range(TT):
                mm = nc.tensor.transpose(tiles(bank(7))[:, t, :], o_tok[:, t, :], ident[:])
            mm.then_inc(a_oT, 1)
            pe.wait_ge(a_oTc, b)
            for t in range(TT):
                mm = nc.tensor.matmul(tiles(bank(5))[:, t, :], oT[:, t * 128:(t + 1) * 128], w["w_out"][:],
                                      start=True, stop=True)
            mm.then_inc(a_y, 1)

        def a_project_q(pe, n):
            pe.wait_ge(na.xT_ready, n + 1)
            pe.wait_ge(a_prod, 4 * n - 2)
            nc.tensor.matmul(bank(0), w["w_qkv"][:, 0:D], xT[:], start=True, stop=True)
            nc.tensor.matmul(bank(1), w["w_qk_rot"][:, 0:D], xT[:], start=True, stop=True).then_inc(a_q, 1)

        def a_tensor_step(pe, b, ending=True):
            pe.wait_ge(a_prod, 4 * b)
            pe.wait_ge(a_v, b)
            for n, weight in ((2, w["w_qkv"][:, D:2 * D]), (3, w["w_qk_rot"][:, D:2 * D]), (4, w["w_qkv"][:, 2 * D:3 * D])):
                for t in range(TT):
                    mm = nc.tensor.matmul(tiles(bank(n))[:, t, :], xT[:, t * 128:(t + 1) * 128], weight,
                                          start=True, stop=True)
            mm.then_inc(a_kv, 1)
            if ending:
                pe.wait_ge(a_oTc, b - 1)
            na.tensor_turn(pe, b + 1, 7)
            if ending:
                pe.wait_ge(a_x, b - 1)
                a_sums(pe, b)
                a_numerators(pe, b)
            a_project_q(pe, b + 1)
            if ending:
                a_output(pe, b)

        def attn_a_tensor(pe):
            na.tensor_turn(pe, 1, 7)
            a_project_q(pe, 1)
            a_tensor_step(pe, 1, ending=False)
            with pe.Fori(2, B + 1) as b:
                a_tensor_step(pe, b)
            pe.wait_ge(a_x, B)
            a_sums(pe, B + 1)
            a_numerators(pe, B + 1)
            a_output(pe, B + 1)

        def a_keep_heads(v, b):
            v.wait_ge(a_sum, b)
            v.wait_ge(a_num, b - 1)
            nc.vector.tensor_tensor(kv_bd[:, 0:D], bank(5, D), const["same_head"][:], ALU.mult).then_inc(a_bd, 1)
            nc.vector.tensor_scalar(kv_bd[:, D:D + H], const["head_mask"][:], psum[:, 5, D:D + 1], None,
                                    ALU.mult).then_inc(a_bd, 1)

        def a_divide(v, b):
            v.wait_ge(a_num, b)
            nc.vector.tensor_scalar(den[:], num_den(5)[:, :, D:D + H], EPS, None, ALU.max).then_inc(a_den, 1)
            v.wait_ge(a_den, b)
            nc.vector.reciprocal(rec[:], den[:]).then_inc(a_rec, 1)
            v.wait_ge(a_rec, b)
            v.wait_ge(a_oT, b - 1)
            nc.vector.tensor_tensor(o_tok[:].rearrange("p t (h d) -> p t h d", d=HD),
                                    num_den(5)[:, :, 0:D].rearrange("p t (h d) -> p t h d", d=HD),
                                    rec[:].unsqueeze(3).broadcast_to([128, TT, H, HD]),
                                    ALU.mult).then_inc(a_o, 1)

        def a_add(v, b):
            v.wait_ge(a_y, b)
            nc.vector.tensor_tensor(xs(b - 1, 0, TT), bank(5), xs(b - 1, 0, TT), ALU.add).then_inc(a_x, 1)

        def a_rotate(v, b, n, prod, first_bank, table):
            v.wait_ge(a_feat, 2 * b + n - 1)
            for m in range(2):
                nc.vector.tensor_tensor(prod[:, m, :], bank(first_bank + m), table[:, m, :], ALU.mult).then_inc(a_prod, 1)
            v.wait_ge(a_prod, 4 * b + 2 * n + 2)
            nc.vector.tensor_tensor(prod[:, 0, :], prod[:, 0, :], prod[:, 1, :], ALU.add).then_inc(a_rope, 1)
            v.wait_ge(a_rope, 2 * b + n + 1)
            nc.vector.tensor_scalar((q_exp, k_exp)[n], prod[:, 0, :], 0.0, None, ALU.min).then_inc(a_min, 1)

        def a_feature(v, b, n, prod, e, feat):
            v.wait_ge(a_exp, 2 * b + n + 1)
            v.wait_ge((a_num, a_sum)[n], b)
            nc.vector.scalar_tensor_tensor(feat, prod[:, 0, :], 0.0, e, ALU.max, ALU.add).then_inc(a_feat, 1)

        def a_rotate_q(v, n):
            v.wait_ge(a_q, n + 1)
            a_rotate(v, n, 0, q_prod, 0, rope_q)

        def a_vector_step(v, b, ending=True):
            na.vector_hat(v, b + 1)
            if ending:
                a_keep_heads(v, b)
            v.wait_ge(a_kv, b + 1)
            a_rotate(v, b, 1, k_prod, 2, rope_k)
            if ending:
                a_divide(v, b)
            a_feature(v, b, 0, q_prod, q_exp, q_feat)
            na.vector_stats(v, b + 2)
            a_feature(v, b, 1, k_prod, k_exp, k_feat)
            a_rotate_q(v, b + 1)
            if ending:
                a_add(v, b)

        def attn_a_vector(v):
            na.vector_stats(v, 1)
            na.vector_hat(v, 1)
            v.wait_ge(loaded_first, 16 * len(first_loads))
            a_rotate_q(v, 1)
            v.wait_ge(loaded_x, 16 * (B - 1))
            na.vector_stats(v, 2)
            a_vector_step(v, 1, ending=False)
            with v.Fori(2, B + 1) as b:
                a_vector_step(v, b)
            a_keep_heads(v, B + 1)
            v.wait_ge(na.rstd_ready, B + 3)
            ffn_1.norm.vector_stats(v, 1)
            a_divide(v, B + 1)
            v.wait_ge(na.turned, B + 2)
            ffn_1.norm.vector_hat(v, 1)
            a_add(v, B + 1)

        def a_copy_output(a, b):
            a.wait_ge(a_oT, b)
            a.wait_ge(a_y, b - 1)
            nc.scalar.copy(oT[:], bank(7)).then_inc(a_oTc, 1)

        def a_exponential(a, b, n):
            a.wait_ge(a_min, 2 * b + n + 1)
            e = (q_exp, k_exp)[n]
            nc.scalar.activation(e, e, ACT.Exp).then_inc(a_exp, 1)

        def a_scalar_step(a, b, ending=True):
            a.wait_ge(a_kv, b + 1)
            a.wait_ge(a_sum, b)
            nc.scalar.copy(v_ones[:, :, 0:D], tiles(bank(4))).then_inc(a_v, 1)
            na.scalar_copy(a, b + 1, 7)
            a_exponential(a, b, 1)
            if ending:
                a_copy_output(a, b)
            a_exponential(a, b + 1, 0)

        def attn_a_scalar(a):
            na.scalar_copy(a, 1, 7)
            a_exponential(a, 1, 0)
            a_scalar_step(a, 1, ending=False)
            with a.Fori(2, B + 1) as b:
                a_scalar_step(a, b)
            a_copy_output(a, B + 1)

        def attn_a_pool(p):
            columns = E * INNER
            piece = columns // B
            assert piece * B == columns
            na.pool_rstd(p, 1)
            na.pool_rstd(p, 2)
            with p.Fori(1, B + 1) as b:
                na.pool_rstd(p, b + 2)
                p.wait_ge(loaded, 16 * len(rest_loads))
                for g, name in enumerate(("w_gate", "w_up")):
                    whole = w[name][:, bass.ds((b - 1) * piece, piece)]
                    high, low = (stacks[:, bass.ds((2 * g + a) * columns + (b - 1) * piece, piece)] for a in range(2))
                    nc.gpsimd.tensor_copy(high, whole).then_inc(split_high, 1)
                    p.wait_ge(split_high, 2 * b + g - 1)
                    p.sem_inc(split_go, 1)
                    nc.gpsimd.tensor_tensor(low, whole, high.bitcast(F32), ALU.subtract).then_inc(split_low, 1)

        split_high, split_low, split_go = sem("split_high"), sem("split_low"), sem("split_go")

        silu_out = ring_a[:, 0:IC * T].rearrange("p (c n) -> p c n", c=IC)
        hidden = ring_a[:, IC * T:3 * IC * T].rearrange("p (e c n) -> p e c n", e=2, c=IC)
        w_parts = stacks[:, 0:4 * E * INNER].rearrange("p (g a e c n) -> p g a e c n", g=2, a=2, e=E, c=IC)
        w_whole = [w[k][:].rearrange("p (e c n) -> p e c n", e=E, c=IC) for k in ("w_gate", "w_up")]
        PRODUCTS = ((0, 0), (0, 1), (1, 0))
        w_down = w["w_down"][:].rearrange("p (e c n) -> p e c n", e=E, c=IC)
        by_expert = lambda ap: ap.rearrange("p (t e) -> p t e", e=ROUTED)
        spread = lambda ap: ap.unsqueeze(2).broadcast_to([128, TT, ROUTED])
        EC = E * IC
        XC = 1 + ROUTED * TT
        LINKS = 17

        class Experts:
            def __init__(self, name, previous, is_split):
                self.previous, self.is_split = previous, is_split
                self.logits, self.gate_up, self.y = signals("tensor", name, logits=1, gate_up=EC, y=E)
                self.logit_ready, self.chain, self.weight_ready, self.hidden, self.x = signals(
                    "vector", name, logit_ready=1, chain=LINKS, weight_ready=1, hidden=EC, x=XC)
                self.exp_ready, self.silu, self.x_high = signals("scalar", name, exp_ready=1, silu=EC, x_high=1)
                self.x_low, = signals("vector", name, x_low=1)
                self.w_high, self.w_low = signals("scalar", name, passed=0, w_high=1)[0], signals(
                    "vector", name, passed=0, w_low=1)[0]
                self.norm = Norm(name, self.logits, 1)
                self.done = (self.x, (B + 1) * XC, self.norm, B + 2)

            def tensor_turn(self, pe, n):
                pe.wait_ge(self.x_low, n)
                self.norm.tensor_turn(pe, n, 6)

            def tensor_logits(self, pe, n):
                pe.wait_ge(self.norm.xT_ready, n + 1)
                pe.wait_ge(self.logit_ready, n)
                for t in range(TT):
                    mm = nc.tensor.matmul(psum[:, 7, t * ROUTED:(t + 1) * ROUTED], xT[:, t * 128:(t + 1) * 128],
                                          w["w_router"][:], start=True, stop=True)
                mm.then_inc(self.logits, 1)

            def tensor(self, pe):
                after(pe, self.previous)
                self.tensor_turn(pe, 1)
                if self.is_split:
                    pe.wait_ge(split_low, 2 * B)
                else:
                    pe.wait_ge(self.w_low, 2 * E)
                self.tensor_logits(pe, 1)
                with pe.Fori(1, B + 1) as b:
                    pe.wait_ge(self.x_high, b + 1)
                    pe.wait_ge(self.x_low, b + 1)
                    for e in range(E + 1):
                        if e < E:
                            for c in range(IC):
                                pe.wait_ge(self.hidden, b * EC + max(e * IC + c - 1, 0))
                                for g in range(2):
                                    for n, (wp, xp) in enumerate(PRODUCTS):
                                        mm = nc.tensor.matmul(bank(2 * g + c), w_parts[:, g, wp, e, c, :],
                                                              (x_high, x_low)[xp], start=n == 0, stop=n == 2)
                                mm.then_inc(self.gate_up, 1)
                        if e == E - 1:
                            self.tensor_turn(pe, b + 1)
                        if e > 0:
                            pe.wait_ge(self.hidden, b * EC + e * IC)
                            done = 0 if e < 3 else 1 + (e - 3) * TT
                            pe.wait_ge(self.x, b * XC + done)
                            for t in range(TT):
                                for c in range(IC):
                                    mm = nc.tensor.matmul(tiles(bank(4 + (e - 1) % 2))[:, t, :],
                                                          hidden[:, (e - 1) % 2, c, t * 128:(t + 1) * 128],
                                                          w_down[:, e - 1, c, :], start=c == 0, stop=c == IC - 1)
                            mm.then_inc(self.y, 1)
                        if e == E - 1:
                            self.tensor_logits(pe, b + 1)

            def scalar_parts(self, a, n):
                self.norm.scalar_copy(a, n, 6)
                a.wait_ge(self.gate_up, n * EC)
                nc.scalar.copy(x_high, bank(6)).then_inc(self.x_high, 1)
                a.wait_ge(self.logit_ready, n + 1)
                nc.scalar.activation(route[:, 0], logit[:], ACT.Exp, scale=-1.0).then_inc(self.exp_ready, 1)

            def scalar(self, a):
                after(a, self.previous)
                self.scalar_parts(a, 1)
                with a.Fori(1, B + 1) as b:
                    for e in range(E):
                        for c in range(IC):
                            a.wait_ge(self.gate_up, b * EC + e * IC + c + 1)
                            a.wait_ge(self.hidden, b * EC + max(e * IC + c - 1, 0))
                            nc.scalar.activation(silu_out[:, c, :], bank(c), ACT.Silu).then_inc(self.silu, 1)
                    self.scalar_parts(a, b + 1)

            def pool(self, p):
                self.norm.pool_rstd(p, 1)
                after(p, self.previous)
                with p.Fori(1, B + 1) as b:
                    self.norm.pool_rstd(p, b + 1)

            def routing(self, v, b, links):
                for n in links:
                    if n == 0:
                        v.wait_ge(self.exp_ready, b + 1)
                    else:
                        v.wait_ge(self.chain, b * LINKS + n)
                    prob, first, second, score = (route[:, k] for k in range(1, 5))
                    left = route[:, 5]
                    rank = by_expert(const["choice_rank"][:])
                    k, (source, chosen) = (0, (prob, first)) if n < 9 else (3, (left, second))
                    tt = nc.vector.tensor_tensor
                    if n == 0:
                        ins = nc.vector.tensor_scalar(score, route[:, 0], 1.0, None, ALU.add)
                    elif n == 1:
                        ins = nc.vector.reciprocal(prob, score)
                    elif n in (2, 8):
                        if n == 8:
                            k, source = 3, left
                        ins = nc.vector.tensor_reduce(best[:, k], source, AX.X, ALU.max)
                    elif n in (3, 9):
                        ins = tt(score, source, spread(best[:, k]), ALU.is_equal)
                    elif n in (4, 10):
                        ins = tt(score, score, rank, ALU.mult)
                    elif n in (5, 11):
                        ins = nc.vector.tensor_reduce(best[:, k + 1], score, AX.X, ALU.max)
                    elif n in (6, 12):
                        ins = tt(chosen, score, spread(best[:, k + 1]), ALU.is_equal)
                    elif n == 7:
                        ins = nc.vector.scalar_tensor_tensor(left, first, -2.0, prob, ALU.mult, ALU.add)
                    elif n == 13:
                        ins = tt(best[:, 2], best[:, 0], best[:, 3], ALU.add)
                    elif n == 14:
                        ins = nc.vector.reciprocal(best[:, 5], best[:, 2])
                    elif n == 15:
                        ins = tt(score, first, second, ALU.add)
                    elif n == 16:
                        ins = tt(score, score, prob, ALU.mult)
                    else:
                        tt(gate_weight[:], score, spread(best[:, 5]), ALU.mult).then_inc(self.weight_ready, 1)
                        continue
                    ins.then_inc(self.chain, 1)

            def split_high(self, a, experts):
                for e in experts:
                    for g in range(2):
                        nc.scalar.copy(w_parts[:, g, 0, e], w_whole[g][:, e]).then_inc(self.w_high, 1)

            def split_low(self, v, experts):
                for e in experts:
                    for g in range(2):
                        v.wait_ge(self.w_high, 2 * e + g + 1)
                        nc.vector.tensor_tensor(w_parts[:, g, 1, e], w_whole[g][:, e], w_parts[:, g, 0, e].bitcast(F32),
                                                ALU.subtract).then_inc(self.w_low, 1)

            def vector_parts(self, v, n):
                v.wait_ge(self.x_high, n + 1)
                nc.vector.tensor_tensor(x_low, bank(6), x_high.bitcast(F32), ALU.subtract).then_inc(self.x_low, 1)
                v.wait_ge(self.logits, n + 1)
                v.wait_ge(self.exp_ready, n)
                nc.vector.tensor_tensor(logit[:], by_expert(bank(7, TT * ROUTED)), by_expert(w["router_bias"][:]),
                                        ALU.add).then_inc(self.logit_ready, 1)

            def vector(self, v):
                after(v, self.previous)
                self.vector_parts(v, 1)
                with v.Fori(1, B + 1) as b:
                    for e in range(E + 1):
                        if e < E:
                            for c in range(IC):
                                v.wait_ge(self.silu, b * EC + e * IC + c + 1)
                                if c == 0:
                                    v.wait_ge(self.y, b * E + max(e - 1, 0))
                                nc.vector.tensor_tensor(hidden[:, e % 2, c, :], bank(2 + c), silu_out[:, c, :],
                                                        ALU.mult).then_inc(self.hidden, 1)
                                if e < 2:
                                    n = e * IC + c
                                    self.routing(v, b, range((LINKS + 1) * n // 4, (LINKS + 1) * (n + 1) // 4))
                        if e == 4:
                            self.norm.vector_stats(v, b + 1)
                        if e == 6:
                            self.norm.vector_hat(v, b + 1)
                        if e > 0:
                            v.wait_ge(self.y, b * E + e)
                            y = tiles(bank(4 + (e - 1) % 2))
                            if e == 1:
                                nc.vector.tensor_tensor(xs(b, 0, TT), bank(4), xs(b, 0, TT), ALU.add).then_inc(self.x, 1)
                                v.wait_ge(self.weight_ready, b + 1)
                                continue
                            v.wait_ge(self.x, b * XC + 1 + (e - 2) * TT)
                            for t in range(TT):
                                nc.vector.scalar_tensor_tensor(xs(b, t), y[:, t, :], gate_weight[:, t, e - 2:e - 1],
                                                               xs(b, t), ALU.mult, ALU.add).then_inc(self.x, 1)
                        if e == E - 1:
                            self.vector_parts(v, b + 1)

        UNITS = [(k, k) for k in range(TT)] + [(k, q) for k in range(TT) for q in range(k + 1, TT)]
        NA, NB = 2 * TT, len(UNITS) // 2
        KA, KB = NA * GROUPS, NB * GROUPS
        TICKS = "B0 A0 A1 B1 B2 A2 A3 A4 B3 A5 B4 A6 A7".split()
        NT = len(TICKS)
        assert [t for t in TICKS if t[0] == "A"] == [f"A{i}" for i in range(NA)]
        A_STEPS = [(1, 0), (1, 1), (3, 0), (0, 0), (3, 1), (0, 1), (2, 1), (2, 0)]
        BUILD = {0: 0, 7: 1, 11: 2}
        STACKED = {2: 0, 9: 1, 12: 2}
        HALVES = {1: (-1, 3, 0), 2: (-1, 3, 1), 3: (-1, 4, 0), 4: (-1, 4, 1), 5: (0, 0, 0),
                  6: (0, 0, 1), 8: (0, 1, 0), 10: (0, 1, 1), 11: (0, 2, 0), 12: (0, 2, 1)}
        LOGS = {2: 0, 5: 1, 8: 2, 11: 3}
        POOL_STEPS = "Q0 B0 B1 Q1 Q2 Q3".split()
        COPY_Q = 3
        TURN_R = (7, 3, 2, 3)
        POOL_FROM = 1
        RING = 4
        head_q = stacks[:, 0:H * T].rearrange("p (h n) -> p h n", h=H)
        stack_ky = stacks[:, H * T:(H + 2) * T].rearrange("p (g n) -> p g n", g=2)
        stack_k = stacks[:, (H + 2) * T:].rearrange("p (g n) -> p g n", g=GROUPS)
        high, stack_q = x_high, x_low
        minus_low = sb("minus_low_r", [128, 2, 128], F32R)
        exps = ring_a[:].rearrange("p (r a n) -> p r a n", r=RING, a=2)
        ring = ring_b[:].rearrange("p (r n) -> p r n", r=RING)
        half_sums = sb("half_sums", [OW, 2, T])
        exp_sums, exp_sums_eps, r_tok = (sb(k, [128, TT, 4]) for k in ("exp_sums", "exp_sums_eps", "r_tok"))
        r_rowsT = sb("r_rowsT", [TT * 4, 128])

        def first_bank(s, t, parts):
            if not parts.stage_b:
                return 2 * (int(TICKS[t][1]) % 2)
            if not parts.stage_a:
                return 2 * ((s * NB + int(TICKS[t][1])) % 2)
            return 2 * ((s * NT + t) % 2)

        class Parts:

            def __init__(self, stage_b=True, stage_a=True, chain=True, build=True, ending=True, ahead=True):
                self.stage_b, self.stage_a, self.chain, self.build = stage_b, stage_a, chain, build
                self.ending, self.ahead = ending, ahead

        LEAD_IN = (Parts(False, False, False), Parts(False, True, False), Parts(False))
        FIRST = (Parts(ending=False),) * GROUPS
        MIDDLE = (Parts(),) * GROUPS
        LAST = (Parts(ahead=False), Parts(build=False, ahead=False), Parts(stage_a=False, build=False, ahead=False),
                Parts(stage_a=False, chain=False, build=False, ahead=False))

        class LogAttention:
            def __init__(self, previous):
                self.previous = previous
                (self.v_product, self.b_score, self.sum_b, self.num, self.oT, self.y) = signals(
                    "tensor", "b", v_product=1, b_score=KB, sum_b=KB, num=2, oT=1, y=1)
                self.a_score, = signals("tensor", "b", passed=1 / 2, a_score=KA)
                self.r_turned, = signals("tensor", "b", passed=3 / 4, r_turned=4)
                self.stack_product, self.stack_low = signals(
                    "tensor", "b", passed=1 / 4, stack_product=3 * GROUPS, stack_low=3 * GROUPS)
                (self.v_ready, self.ratio, self.den, self.rec, self.o, self.x) = signals(
                    "vector", "b", v_ready=2, ratio=KB, den=2, rec=2, o=2, x=1)
                self.exp_sum, = signals("vector", "b", passed=1 / 2, exp_sum=2 * KA)
                self.sum_eps, self.r_ready = signals("vector", "b", passed=3 / 4, sum_eps=4, r_ready=4)
                self.head_q, = signals("vector", "b", passed=1 / 4, head_q=POOL_FROM * GROUPS)
                self.head_q_pool, = signals("pool", "b", passed=1 / 4, head_q_pool=(4 - POOL_FROM) * GROUPS)
                self.abs, self.ln, self.half_ready, self.oTc = signals(
                    "scalar", "b", abs=KB, ln=KB, half_ready=2, oTc=1)
                self.exp, = signals("scalar", "b", passed=1 / 2, exp=KA)
                self.r_copied, = signals("scalar", "b", passed=3 / 4, r_copied=4)
                self.high, self.stack = signals("scalar", "b", passed=1 / 4, high=3 * GROUPS, stack=3 * GROUPS)
                self.table_ready = sem("b_table_ready")
                self.mask_b, = signals("pool", "b", mask_b=2 * GROUPS)
                self.stored, self.spread = sem("b_stored"), sem("b_spread")
                self.zeroed = sem("b_zeroed")
                self.norm = Norm("b", self.stack_product, 3 * GROUPS, 3 * (GROUPS - 1))
                self.go, self.sync_go = sem("b_mask_go"), sem("b_sync_go")
                self.done = (self.x, B + 1, self.norm, B + 1)

            def spreads(self, b, s):
                return 16 * (4 * (b - 1) + s + 2)

            def build_product(self, pe, b, s, piece):
                if (s, piece) == (2, 1):
                    pe.wait_ge(self.x, b)
                if (s, piece) == (1, 0):
                    pe.wait_ge(self.norm.xT_ready, b + 2)
                pe.wait_ge(self.stack, b * 3 * GROUPS + 3 * s + piece)
                g = (s + 3) % GROUPS
                weight = w[("b_q", "b_ky", "b_k")[piece]]
                nc.tensor.matmul(bank(4), weight[:, g * 128:(g + 1) * 128], xT[:], start=True,
                                 stop=True).then_inc(self.stack_product, 1)

            def subtract_high(self, pe, b, s, piece):
                pe.wait_ge(self.high, b * 3 * GROUPS + 3 * s + piece + 1)
                nc.tensor.matmul(bank(4), minus_low[:, min(piece, 1), :], high, start=False, stop=True,
                                 skip_group_check=True).then_inc(self.stack_low, 1)

            def score(self, pe, b, s, t, parts):
                n = s * NT + t
                kind, i = TICKS[t][0], int(TICKS[t][1])
                alone = not (parts.stage_a and parts.stage_b)
                if not parts.stage_b:
                    pe.wait_ge(self.exp, b * KA + s * NA + i - 1)
                elif alone:
                    pe.wait_ge(self.abs, b * KB + s * NB + (i if s == 2 and i < 2 else i - 1))
                    if s == 2 and i == 0:
                        pe.wait_ge(self.exp, b * KA + s * NA)
                before = n - 2
                bs, bt = divmod(before % (GROUPS * NT), NT)
                wrapped = before < 0
                bk, bi = TICKS[bt][0], int(TICKS[bt][1])
                if alone:
                    pass
                elif bk == "A":
                    pe.wait_ge(self.exp, b * KA + bs * NA + bi + 1 - (KA if wrapped else 0))
                else:
                    pe.wait_ge(self.abs, b * KB + bs * NB + bi + 1 - (KB if wrapped else 0))
                if s == 0 and t < 2:
                    pe.wait_ge(self.exp, b * KA)
                first = first_bank(s, t, parts)
                if kind == "A":
                    g, (qb, pair) = (s + 2) % GROUPS, A_STEPS[i]
                    if i == 0:
                        pe.wait_ge(self.stack, b * 3 * GROUPS + 3 * s)
                        if POOL_FROM > 0:
                            pe.wait_ge(self.head_q, (b * GROUPS + s) * POOL_FROM)
                        pe.wait_ge(self.head_q_pool, (b * GROUPS + s) * (4 - POOL_FROM))
                    for h in range(2):
                        mm = nc.tensor.matmul(bank(first + h, (qb + 1) * 128),
                                              head_q[:, 4 * g + 2 * pair + h, qb * 128:(qb + 1) * 128],
                                              stack_ky[:, (s + 1) % 2, 0:(qb + 1) * 128], start=True, stop=True)
                    mm.then_inc(self.a_score, 1)
                else:
                    for m, (kb, qb) in enumerate(UNITS[2 * i:2 * i + 2]):
                        mm = nc.tensor.matmul(bank(first + m), stack_k[:, s, kb * 128:(kb + 1) * 128],
                                              head_q[:, 4 * s:4 * s + 4, qb * 128:(qb + 1) * 128],
                                              start=True, stop=True)
                    mm.then_inc(self.b_score, 1)

            def weighted_values(self, pe, b, s, i, m):
                if (s % 2, i, m) == (0, 0, 0):
                    half = s // 2
                    pe.wait_ge(self.v_ready, 2 * b + half + 1)
                    pe.wait_ge(self.half_ready, 2 * b + half - 1)
                if m == 0 and i < 2:
                    pe.wait_ge(self.mask_b, b * 2 * GROUPS + 2 * s + i + 1)
                elif m == 0:
                    pe.wait_ge(self.ln, b * KB + s * NB + i + 1)
                first, last = s % 2 == 0 and i == 0, s % 2 == 1 and i == NB - 1
                kb, qb = UNITS[2 * i + m]
                for h in range(4):
                    mm = nc.tensor.matmul(psum[0:OW, 5 + s % GROUPS // 2, qb * 128:(qb + 1) * 128],
                                          values[:, kb, 4 * (s % GROUPS) + h, :],
                                          ring[:, (s * NB + i) % RING, m * T + h * 128:m * T + (h + 1) * 128],
                                          start=first and m == 0 and h == 0,
                                          stop=last and m == 1 and h == 3, skip_group_check=True)
                if m == 1:
                    mm.then_inc(self.sum_b, 1)

            def turn_r(self, pe, b, s, ahead):
                pe.wait_ge(self.r_ready, b * 4 + s + 1)
                pe.wait_ge(self.r_copied, b * 4 + s)
                if s == 0:
                    pe.wait_ge(self.v_ready, 2 * b + 2)
                if s == 1 and ahead:
                    pe.wait_ge(self.norm.xT_ready, b + 2)
                if s == 2:
                    pe.wait_ge(self.oTc, b)
                nc.tensor.transpose(psum[0:TT * 4, 7, 0:128], r_tok[:].rearrange("p t h -> p (t h)"),
                                    ident[:]).then_inc(self.r_turned, 1)

            def turn_half(self, pe, b, half, r_copied):
                if half == 0:
                    pe.wait_ge(self.half_ready, 2 * b)
                    pe.wait_ge(self.r_copied, r_copied)
                else:
                    pe.wait_ge(self.o, 2 * b - 1)
                for t in range(TT):
                    mm = nc.tensor.transpose(bank(7)[:, t * OW:(t + 1) * OW], half_sums[:, half, t * 128:(t + 1) * 128],
                                             ident[0:OW, 0:OW])
                mm.then_inc(self.num, 1)

            def turn_output(self, pe, b):
                pe.wait_ge(self.o, 2 * b)
                for t in range(TT):
                    mm = nc.tensor.transpose(tiles(bank(7))[:, t, :], o_tok[:, t, :], ident[:])
                mm.then_inc(self.oT, 1)

            def project(self, pe, b, pieces, end=0):
                pe.wait_ge(self.oTc, b + end)
                pe.wait_ge(self.stack, b * 3 * GROUPS + pieces)
                for t in range(TT):
                    mm = nc.tensor.matmul(tiles(bank(4))[:, t, :], oT[:, t * 128:(t + 1) * 128], w["b_proj"][:],
                                          start=True, stop=True)
                mm.then_inc(self.y, 1)

            def tensor_slot(self, pe, b, s, parts):
                for t, tick in enumerate(TICKS):
                    if (parts.stage_a if tick[0] == "A" else parts.stage_b):
                        self.score(pe, b, s, t, parts)
                    if t in BUILD and parts.build:
                        self.build_product(pe, b, s, BUILD[t])
                    if t in STACKED and parts.build:
                        self.subtract_high(pe, b, s, STACKED[t])
                    if t == TURN_R[s] and parts.chain:
                        self.turn_r(pe, b, s, parts.ahead)
                    if not parts.stage_b:
                        continue
                    if t == 9 and s == 0 and parts.ahead:
                        pe.wait_ge(self.r_copied, b * 4 + 1)
                        self.norm.tensor_turn(pe, b + 1, 7)
                    if t in HALVES:
                        slot, i, m = HALVES[t]
                        if s + slot >= 0 or parts.ending:
                            self.weighted_values(pe, b, s + slot, i, m)
                    if parts.ending and s == 1 and t in (5, 8):
                        self.turn_half(pe, b, {5: 0, 8: 1}[t], 4 * b + 2)
                    if parts.ending and s == 1 and t == 11:
                        self.turn_output(pe, b)
                    if parts.ending and s == 2 and t == 3:
                        self.project(pe, b, 2 * 3 + 1 if parts.build else 3)

            def tensor_batch(self, pe, b, slots):
                pe.wait_ge(self.r_copied, b * 4)
                for t in range(TT):
                    mm = nc.tensor.matmul(tiles(bank(7))[:, t, :], xT[:, t * 128:(t + 1) * 128],
                                          w["b_v"][:], start=True, stop=True)
                mm.then_inc(self.v_product, 1)
                for s, parts in enumerate(slots):
                    self.tensor_slot(pe, b, s, parts)

            def tensor(self, pe):
                after(pe, self.previous)
                self.norm.tensor_turn(pe, 1, 7)
                pe.wait_ge(self.table_ready, 1)
                for s, parts in enumerate(LEAD_IN):
                    self.tensor_slot(pe, 0, s + 1, parts)
                self.tensor_batch(pe, 1, FIRST)
                with pe.Fori(2, B) as b:
                    self.tensor_batch(pe, b, MIDDLE)
                self.tensor_batch(pe, B, LAST)
                for i in (3, 4):
                    for m in range(2):
                        self.weighted_values(pe, B + 1, -1, i, m)
                for half in range(2):
                    self.turn_half(pe, B + 1, half, 4 * B + 3)
                self.turn_output(pe, B + 1)
                self.project(pe, B, 3, end=1)

            def logarithm(self, a, b, s, i):
                a.wait_ge(self.ratio, b * KB + s * NB + i + 1)
                r = ring[:, (s * NB + i) % RING, :]
                nc.scalar.activation(r, r, ACT.Ln, bias=1.0).then_inc(self.ln, 1)

            def scalar_slot(self, a, b, s, parts):
                stage_a, stage_b, ending = parts.stage_a, parts.stage_b, parts.ending
                for t, tick in enumerate(TICKS):
                    kind, i = tick[0], int(tick[1])
                    first = first_bank(s, t, parts)
                    if kind == "A" and stage_a:
                        a.wait_ge(self.a_score, b * KA + s * NA + i + 1)
                        a.wait_ge(self.exp_sum, 2 * (b * KA + s * NA + i + 1 - RING))
                        width = (A_STEPS[i][0] + 1) * 128
                        nc.scalar.activation(exps[:, i % RING, :, 0:width], psum[:, first:first + 2, 0:width],
                                             ACT.Exp, scale=SCALE).then_inc(self.exp, 1)
                    if kind == "B" and stage_b:
                        step = s * NB + i
                        a.wait_ge(self.b_score, b * KB + step + 1)
                        a.wait_ge(self.sum_b, b * KB + step + 1 - RING)
                        nc.scalar.activation(ring[:, step % RING, :].rearrange("p (a n) -> p a n", a=2),
                                             psum[:, first:first + 2, :], ACT.Abs, scale=SCALE).then_inc(self.abs, 1)
                    if t in BUILD and parts.build:
                        a.wait_ge(self.stack_product, b * 3 * GROUPS + 3 * s + BUILD[t] + 1)
                        nc.scalar.copy(high, bank(4)).then_inc(self.high, 1)
                    if t in STACKED and parts.build:
                        self.build_stack(a, b, s, STACKED[t])
                    if t == TURN_R[s] + 1 and parts.chain:
                        a.wait_ge(self.r_turned, b * 4 + s + 1)
                        if stage_b:
                            a.wait_ge(self.stored, self.spreads(b, s) - 16)
                        nc.scalar.copy(r_rowsT[:], psum[0:TT * 4, 7, 0:128]).then_inc(self.r_copied, 1)
                    if not stage_b:
                        continue
                    if t == 0 and (s > 0 or ending):
                        self.logarithm(a, b, s - 1, NB - 1)
                    if t in LOGS:
                        self.logarithm(a, b, s, LOGS[t])
                    if t == 12 and s == 0 and parts.ahead:
                        self.norm.scalar_copy(a, b + 1, 7)
                    if t == 7 and s == 2:
                        self.copy_half(a, b, 0)
                    if ending and t == 5 and s == 0:
                        self.copy_half(a, b - 1, 1)
                    if ending and t == 12 and s == 1:
                        self.copy_output(a, b)

            def build_stack(self, a, b, s, piece):
                a.wait_ge(self.stack_low, b * 3 * GROUPS + 3 * s + piece + 1)
                if piece == 0:
                    a.wait_ge(self.head_q, (b * GROUPS + s) * POOL_FROM)
                    a.wait_ge(self.head_q_pool, (b * GROUPS + s) * (4 - POOL_FROM))
                if piece == 1:
                    a.wait_ge(self.a_score, b * KA + s * NA)
                if piece == 2:
                    a.wait_ge(self.b_score, b * KB + s * NB)
                out = (stack_q, stack_ky[:, s % 2, :], stack_k[:, (s + 3) % GROUPS, :])[piece]
                nc.scalar.copy(out, bank(4)).then_inc(self.stack, 1)

            def copy_half(self, a, b, half):
                a.wait_ge(self.sum_b, b * KB + (half + 1) * KB // 2)
                a.wait_ge(self.num, 2 * b)
                nc.scalar.copy(half_sums[:, half, :], psum[0:OW, 5 + half, :]).then_inc(self.half_ready, 1)

            def copy_output(self, a, b):
                a.wait_ge(self.oT, b)
                a.wait_ge(self.y, b - 1)
                nc.scalar.copy(oT[:], bank(7)).then_inc(self.oTc, 1)

            def scalar(self, a):
                after(a, self.previous)
                nc.scalar.preload_act_table_set("natural_log_exp_and_others")
                self.norm.scalar_copy(a, 1, 7)
                nc.scalar.copy(minus_low[:].rearrange("p a n -> p (a n)"), const["minus_low"][:]).then_inc(self.table_ready, 1)
                for s, parts in enumerate(LEAD_IN):
                    self.scalar_slot(a, 0, s + 1, parts)
                for s, parts in enumerate(FIRST):
                    self.scalar_slot(a, 1, s, parts)
                with a.Fori(2, B) as b:
                    for s, parts in enumerate(MIDDLE):
                        self.scalar_slot(a, b, s, parts)
                for s, parts in enumerate(LAST):
                    self.scalar_slot(a, B, s, parts)
                self.logarithm(a, B + 1, -1, NB - 1)
                self.copy_half(a, B, 1)
                a.wait_ge(self.b_score, (B + 1) * KB)
                ffn_2.split_high(a, range(0, E // 2))
                self.copy_output(a, B + 1)
                ffn_2.split_high(a, range(E // 2, E))

            def copy_first_q(self, v, b, s):
                v.wait_ge(self.stack, b * 3 * GROUPS + 3 * s + 1)
                v.wait_ge(self.b_score, b * KB + s * NB)
                for j in range(POOL_FROM):
                    rows = slice(32 * j, 32 * (j + 1))
                    nc.vector.tensor_copy(head_q[rows, 4 * ((s + 3) % GROUPS) + j, :], stack_q[rows, :].bitcast(F32)
                                          ).then_inc(self.head_q, 1)

            def sum_exps(self, v, b, s, i):
                qb, pair = A_STEPS[i]
                width = (qb + 1) * 128
                v.wait_ge(self.exp, b * KA + s * NA + i + 1)
                for h in range(2):
                    e = exps[:, i % RING, h, 0:width]
                    nc.vector.scalar_tensor_tensor(e, e, CLIP_LO, const["upper"][:, T - width:T], ALU.max, ALU.min,
                                                   accum_out=exp_sums[:, qb, 2 * pair + h:2 * pair + h + 1]
                                                   ).then_inc(self.exp_sum, 1)

            def copy_values(self, v, b, half):
                for t in range(TT):
                    dst = diagonal(values[:, t, half * HALF:(half + 1) * HALF, :].rearrange("p h n -> p (h n)"))
                    ins = nc.vector.tensor_copy(dst, psum[:, 7, t * D + half * HALF * HD:t * D + (half + 1) * HALF * HD]
                                                .rearrange("p (h d) -> p h d", d=HD))
                ins.then_inc(self.v_ready, 1)

            def divide(self, v, b, half):
                n = 2 * b + half - 1
                turned = bank(7, TT * OW).rearrange("p (t n) -> p t n", t=TT)
                lo, hi = half * HALF, (half + 1) * HALF
                v.wait_ge(self.num, n)
                nc.vector.tensor_scalar(den[:, :, lo:hi], turned[:, :, HALF * HD:OW], EPS, None, ALU.add
                                        ).then_inc(self.den, 1)
                v.wait_ge(self.den, n)
                nc.vector.reciprocal(rec[:, :, lo:hi], den[:, :, lo:hi]).then_inc(self.rec, 1)
                v.wait_ge(self.rec, n)
                v.wait_ge(self.oT, b - 1)
                nc.vector.tensor_tensor(
                    o_tok[:, :, lo * HD:hi * HD].rearrange("p t (h d) -> p t h d", d=HD),
                    turned[:, :, 0:HALF * HD].rearrange("p t (h d) -> p t h d", d=HD),
                    rec[:, :, lo:hi].unsqueeze(3).broadcast_to([128, TT, HALF, HD]),
                    ALU.mult).then_inc(self.o, 1)

            def add_output(self, v, b):
                v.wait_ge(self.y, b)
                nc.vector.tensor_tensor(xs(b - 1, 0, TT), bank(4), xs(b - 1, 0, TT), ALU.add).then_inc(self.x, 1)

            def vector_slot(self, v, b, s, parts):
                stage_a, stage_b, ending = parts.stage_a, parts.stage_b, parts.ending
                if parts.chain:
                    v.wait_ge(self.exp_sum, 2 * (b * KA + s * NA))
                    nc.vector.tensor_scalar(exp_sums_eps[:], exp_sums[:], EPS, None, ALU.add).then_inc(self.sum_eps, 1)
                    v.wait_ge(self.sum_eps, b * 4 + s + 1)
                    v.wait_ge(self.r_turned, b * 4 + s)
                    nc.vector.reciprocal(r_tok[:], exp_sums_eps[:]).then_inc(self.r_ready, 1)
                for t, tick in enumerate(TICKS):
                    kind, i = tick[0], int(tick[1])
                    if kind == "A" and stage_a:
                        self.sum_exps(v, b, s, i)
                    if kind == "B" and stage_b:
                        step = s * NB + i
                        v.wait_ge(self.abs, b * KB + step + 1)
                        if i == 0:
                            v.wait_ge(self.spread, self.spreads(b, s) - 16)
                        for m, (kb, qb) in enumerate(UNITS[2 * i:2 * i + 2]):
                            part = ring[:, step % RING, m * T:(m + 1) * T]
                            ins = nc.vector.scalar_tensor_tensor(part, part, EPS, r_rows[:, s % 2, qb * T:(qb + 1) * T],
                                                                 ALU.add, ALU.mult)
                        ins.then_inc(self.ratio, 1)
                    if t == COPY_Q and parts.build:
                        self.copy_first_q(v, b, s)
                    if not stage_b:
                        continue
                    if t == 2 and s == 0 and parts.ahead:
                        self.norm.vector_stats(v, b + 1)
                    if t == 6 and s == 0 and parts.ahead:
                        self.norm.vector_hat(v, b + 1)
                    if t == 4 and s == 0:
                        v.wait_ge(self.sum_b, b * KB)
                        self.copy_values(v, b, 1)
                    if ending and s == 1 and t in (6, 9):
                        self.divide(v, b, {6: 0, 9: 1}[t])
                    if ending and s == 2 and t == 4:
                        self.add_output(v, b)

            def vector(self, v):
                after(v, self.previous)
                self.norm.vector_stats(v, 1)
                self.norm.vector_hat(v, 1)
                v.wait_ge(self.zeroed, 1)
                self.vector_slot(v, 0, 1, LEAD_IN[0])
                v.wait_ge(self.zeroed, 2)
                self.vector_slot(v, 0, 2, LEAD_IN[1])
                v.wait_ge(self.zeroed, GROUPS)
                self.vector_slot(v, 0, 3, LEAD_IN[2])
                self.vector_batch(v, 1, FIRST)
                with v.Fori(2, B) as b:
                    self.vector_batch(v, b, MIDDLE)
                self.vector_batch(v, B, LAST)
                ffn_2.norm.vector_stats(v, 1)
                ffn_2.norm.vector_hat(v, 1)
                for half in range(2):
                    self.divide(v, B + 1, half)
                ffn_2.split_low(v, range(0, E // 2))
                self.add_output(v, B + 1)
                ffn_2.split_low(v, range(E // 2, E))

            def vector_batch(self, v, b, slots):
                v.wait_ge(self.v_product, b + 1)
                v.wait_ge(self.sum_b, b * KB - NB)
                self.copy_values(v, b, 0)
                for s, parts in enumerate(slots):
                    self.vector_slot(v, b, s, parts)

            def copy_q(self, p, b, s, j):
                if j == POOL_FROM:
                    p.wait_ge(self.stack, b * 3 * GROUPS + 3 * s + 1)
                    p.sem_inc(self.go, 1)
                    p.wait_ge(self.b_score, b * KB + s * NB)
                    p.sem_inc(self.go, 1)
                rows = slice(32 * j, 32 * (j + 1))
                nc.gpsimd.tensor_copy(head_q[rows, 4 * ((s + 3) % GROUPS) + j, :], stack_q[rows, :].bitcast(F32)
                                      ).then_inc(self.head_q_pool, 1)

            def pool_slot(self, p, b, s, parts):
                masks, copies = b * 2 * GROUPS + 2 * s, (b * GROUPS + s) * (4 - POOL_FROM)
                if parts.ahead and parts.stage_b and s == 0:
                    self.norm.pool_rstd(p, b + 1)
                for step in POOL_STEPS:
                    kind, i = step[0], int(step[1])
                    if kind == "Q" and i >= POOL_FROM and parts.build:
                        p.wait_ge(self.mask_b, masks)
                        p.sem_inc(self.go, 1)
                        p.wait_ge(self.head_q_pool, copies)
                        p.sem_inc(self.go, 1)
                        self.copy_q(p, b, s, i)
                        copies = copies + 1
                    if kind == "B" and parts.stage_b:
                        if parts.build or s == 1:
                            p.wait_ge(self.head_q_pool, copies)
                            p.sem_inc(self.go, 1)
                        p.wait_ge(self.ln, b * KB + s * NB + i + 1)
                        p.sem_inc(self.go, 1)
                        r = ring[:, (s * NB + i) % RING, :].rearrange("p (u n) -> p u n", n=128)
                        nc.gpsimd.affine_select(out=r, in_=r, pattern=[[0, 8], [1, 128]], compare_op=ALU.is_ge,
                                                fill=0.0, base=0, channel_multiplier=-1).then_inc(self.mask_b, 1)
                        masks = masks + 1

            def pool(self, p):
                after(p, self.previous)
                self.norm.pool_rstd(p, 1)
                for g in range(GROUPS):
                    nc.gpsimd.memset(head_q[:, 4 * g:4 * g + 4, :].bitcast(F32), 0.0).then_inc(self.zeroed, 1)
                p.wait_ge(self.zeroed, GROUPS)
                for s, parts in enumerate(LEAD_IN):
                    self.pool_slot(p, 0, s + 1, parts)
                with p.Fori(1, B) as b:
                    for s, parts in enumerate(MIDDLE):
                        self.pool_slot(p, b, s, parts)
                for s, parts in enumerate(LAST):
                    self.pool_slot(p, B, s, parts)

            def spread_r(self, sp, b, s, first=False):
                if not first:
                    sp.wait_ge(self.spread, self.spreads(b, s) - 16)
                    sp.sem_inc(self.sync_go, 1)
                sp.wait_ge(self.r_copied, b * 4 + s + 1)
                sp.sem_inc(self.sync_go, 1)
                sp.dma_start(dram_r, r_rowsT[:]).then_inc(self.stored, 16)
                sp.wait_ge(self.stored, self.spreads(b, s))
                sp.sem_inc(self.sync_go, 1)
                sp.wait_ge(self.ratio, b * KB + s * NB)
                sp.sem_inc(self.sync_go, 1)
                sp.dma_start(r_rows[:, (s + 1) % 2, :],
                             dram_r.rearrange("h n -> (h n)").unsqueeze(0).broadcast_to([128, GROUPS * T])
                             ).then_inc(self.spread, 16)

            def sync(self, sp):
                after(sp, self.previous)
                self.spread_r(sp, 0, 3, first=True)
                with sp.Fori(1, B) as b:
                    for s in range(GROUPS):
                        self.spread_r(sp, b, s)
                for s in range(GROUPS - 1):
                    self.spread_r(sp, B, s)
                sp.wait_ge(self.spread, 16 * 4 * B)

        def diagonal(ap):
            return bass.AP(ap.tensor, ap.offset, [ap.ap[0], [OW + HD, HALF], [1, HD]])

        ffn_1 = Experts("f1", (a_x, B + 1, na, B + 2), True)
        log_attn = LogAttention(ffn_1.done)
        ffn_2 = Experts("f2", log_attn.done, False)
        stored, store_go = sem("stored"), sem("store_go")

        block = ctx.enter_context(nc.Block())

        @block.sync
        def _(s):
            def load(name, signal):
                dst = {"rope_q": ring_b[:, 0:2 * T], "rope_k": ring_b[:, 2 * T:2 * T + 2 * TT * D]}.get(name)
                if dst is None:
                    dst = (const[name] if name in const else w[name])[:]
                s.dma_start(dst, ins[name]).then_inc(signal, 16)

            for n in range(B):
                if n == 1:
                    for name in first_loads:
                        load(name, loaded_first)
                s.dma_start(tiles(x_res[:, n * TT * D:(n + 1) * TT * D]),
                            x_in[n * T:(n + 1) * T, :].rearrange("(t p) d -> p t d", p=128)
                            ).then_inc(loaded_x0 if n == 0 else loaded_x, 16)
            for name in rest_loads:
                load(name, loaded)
            log_attn.sync(s)
            after(s, log_attn.done)
            with s.Fori(1, B + 1) as b:
                target = out[bass.ds((b - 1) * T, T), :].rearrange("(t p) d -> p t d", p=128)
                source = tiles(xs(b, 0, TT))
                s.wait_ge(ffn_2.x, (b + 1) * XC)
                s.sem_inc(store_go, 1)
                s.dma_start(target, source).then_inc(stored, 16)
            s.wait_ge(stored, 16 * B)

        @block.gpsimd
        def _(p):
            start(p, "pool")
            nc.gpsimd.memset(neg_half[:], -0.5).then_inc(setup, 1)
            nc.gpsimd.memset(x_res[:, B * TT * D:], 0.0).then_inc(setup, 1)
            nc.gpsimd.memset(v_ones[:, :, D:D + 1], 1.0).then_inc(setup, 1)
            nc.gpsimd.memset(values[:], 0.0).then_inc(setup, 1)
            p.wait_ge(setup, 4)
            for half in range(2):
                for t in range(TT):
                    block_of = values[:, t, half * HALF:(half + 1) * HALF, :].rearrange("p h n -> p (h n)")
                    nc.gpsimd.memset(bass.AP(block_of.tensor, block_of.offset + HALF * HD,
                                             [block_of.ap[0], [OW + 1, HALF], [1, 1]]), 1.0).then_inc(setup, 1)
            attn_a_pool(p)
            ffn_1.pool(p)
            log_attn.pool(p)
            ffn_2.pool(p)

        @block.vector
        def _(v):
            start(v, "vector")
            v.wait_ge(setup, SETUP)
            v.wait_ge(loaded_x0, 16)
            attn_a_vector(v)
            v.wait_ge(loaded, 16 * len(rest_loads))
            ffn_1.vector(v)
            log_attn.vector(v)
            ffn_2.vector(v)

        @block.scalar
        def _(a):
            start(a, "scalar")
            a.wait_ge(setup, SETUP)
            attn_a_scalar(a)
            a.wait_ge(loaded, 16 * len(rest_loads))
            ffn_1.scalar(a)
            log_attn.scalar(a)
            ffn_2.scalar(a)

        @block.tensor
        def _(pe):
            start(pe, "tensor")
            pe.wait_ge(setup, SETUP)
            pe.wait_ge(loaded_first, 16 * len(first_loads))
            attn_a_tensor(pe)
            pe.wait_ge(loaded, 16 * len(rest_loads))
            ffn_1.tensor(pe)
            log_attn.tensor(pe)
            ffn_2.tensor(pe)


def lay_out(inputs):
    w_qkv = inputs["L0_attn_a_W_qkv"]
    turned = np.arange(D).reshape(H, 2, HD // 2)[:, ::-1].reshape(-1)

    stacked = np.tile(np.arange(D).reshape(H, 1, HD), (1, PARTS, 1)).reshape(-1)

    def with_shared(shared, routed):
        return np.concatenate([shared[None], routed], 0)

    gate = with_shared(inputs["L0_ffn_sg_w"], inputs["L0_ffn_wg"])
    up = with_shared(inputs["L0_ffn_su_w"], inputs["L0_ffn_wu"])
    down = with_shared(inputs["L0_ffn_sd_w"], inputs["L0_ffn_wd"])
    laid = {
        "w_qkv": w_qkv,
        "w_qk_rot": np.concatenate([w_qkv[:, :D][:, turned], w_qkv[:, D:2 * D][:, turned]], 1),
        "w_out": inputs["L0_attn_a_W_out"],
        "b_q": inputs["L0_attn_b_w_qkv"][:D].T[:, stacked],
        "b_ky": inputs["L0_attn_b_w_ky"].T[:, stacked],
        "b_k": inputs["L0_attn_b_w_qkv"][D:2 * D].T[:, stacked],
        "b_v": inputs["L0_attn_b_w_qkv"][2 * D:].T,
        "b_proj": inputs["L0_attn_b_w_proj"].T,
        "w_gate": gate.transpose(2, 0, 1).reshape(D, -1),
        "w_up": up.transpose(2, 0, 1).reshape(D, -1),
        "w_down": down.reshape(E, D, IC, 128).transpose(3, 0, 2, 1).reshape(128, -1),
        "w_router": inputs["L0_ffn_router_w"].T,
        "router_bias": np.tile(inputs["L0_ffn_routing_bias"], (128, TT)),
    }
    return {k: np.ascontiguousarray(v) for k, v in laid.items()}


def kernel(**inputs):
    from concourse import bacc
    from concourse.bass_utils import run_bass_kernel_spmd

    inputs = {k: np.asarray(v) for k, v in inputs.items()}
    arrays = {"x": np.ascontiguousarray(inputs["L0_attn_a_x"].reshape(B * T, D)), **shape_constants(), **lay_out(inputs)}
    nc = bacc.Bacc("TRN2", target_bir_lowering=False, num_devices=1)
    dram = {k: nc.dram_tensor(f"in_{k}", a.shape, mybir.dt.from_np(a.dtype), kind="ExternalInput").ap()
            for k, a in arrays.items()}
    out = nc.dram_tensor("out", (B * T, D), F32, kind="ExternalOutput").ap()
    build(nc, dram["x"], dram, out)
    result = run_bass_kernel_spmd(nc, [{f"in_{k}": a for k, a in arrays.items()}], core_ids=[0])
    return result.results[0]["out"].reshape(B, T, D)
```
